# Optimizing a Trainium2 kernel written in Bass

```python
import numpy as np
import jax
import jax.numpy as jnp

def _softmax(x, axis=-1):
    return jax.nn.softmax(x, axis=axis)

def _gelu(x):
    return jax.nn.gelu(x, approximate=True)

def _silu(x):
    return jax.nn.silu(x)

def _sigmoid(x):
    return jax.nn.sigmoid(x)

def _layernorm(x, axis=-1, eps=1e-05):
    m = jnp.mean(x, axis=axis, keepdims=True)
    v = jnp.var(x, axis=axis, keepdims=True)
    return (x - m) / jnp.sqrt(v + eps)

def _scatter_add(tgt, idx, src, axis=0):
    return tgt.at[idx].add(src)

def _segment_sum(src, seg, n):
    return jax.ops.segment_sum(src, seg, n)
kernel_name = 'mk_dlrm_tower_d1_rec_r8_7016a3'

def setup_inputs(seed: int=0):
    np.random.seed(seed)
    _w = jnp.asarray

    def _rec_inputs():
        import jax
        import jax.numpy as jnp
        _tk = jax.random.key(seed)
        dense_ctx = jax.random.normal(jax.random.fold_in(_tk, 190), (1024, 16), jnp.float32)
        ids = jnp.stack([jax.random.randint(jax.random.fold_in(_tk, 200 + f), (1024,), 0, v, jnp.int32) for f, v in enumerate([1250, 1000, 12500, 1250, 125000, 12500, 1250, 1250, 1250, 1250, 1000, 1250, 1000, 125000, 1000, 125000, 1250, 1250, 12500, 125000, 12500, 12500, 1250, 1000, 1250, 1000, 1250, 125000, 12500, 1000, 1000, 1000, 12500, 1250, 1250, 125000, 125000, 1250, 1000])], axis=1)
        tbl_0 = 0.05 * jax.random.normal(jax.random.fold_in(_tk, 500 + 0), (1250, 16), jnp.float32)
        tbl_1 = 0.05 * jax.random.normal(jax.random.fold_in(_tk, 500 + 1), (1000, 16), jnp.float32)
        tbl_2 = 0.05 * jax.random.normal(jax.random.fold_in(_tk, 500 + 2), (12500, 16), jnp.float32)
        tbl_3 = 0.05 * jax.random.normal(jax.random.fold_in(_tk, 500 + 3), (1250, 16), jnp.float32)
        tbl_4 = 0.05 * jax.random.normal(jax.random.fold_in(_tk, 500 + 4), (125000, 16), jnp.float32)
        tbl_5 = 0.05 * jax.random.normal(jax.random.fold_in(_tk, 500 + 5), (12500, 16), jnp.float32)
        tbl_6 = 0.05 * jax.random.normal(jax.random.fold_in(_tk, 500 + 6), (1250, 16), jnp.float32)
        tbl_7 = 0.05 * jax.random.normal(jax.random.fold_in(_tk, 500 + 7), (1250, 16), jnp.float32)
        tbl_8 = 0.05 * jax.random.normal(jax.random.fold_in(_tk, 500 + 8), (1250, 16), jnp.float32)
        tbl_9 = 0.05 * jax.random.normal(jax.random.fold_in(_tk, 500 + 9), (1250, 16), jnp.float32)
        tbl_10 = 0.05 * jax.random.normal(jax.random.fold_in(_tk, 500 + 10), (1000, 16), jnp.float32)
        tbl_11 = 0.05 * jax.random.normal(jax.random.fold_in(_tk, 500 + 11), (1250, 16), jnp.float32)
        tbl_12 = 0.05 * jax.random.normal(jax.random.fold_in(_tk, 500 + 12), (1000, 16), jnp.float32)
        tbl_13 = 0.05 * jax.random.normal(jax.random.fold_in(_tk, 500 + 13), (125000, 16), jnp.float32)
        tbl_14 = 0.05 * jax.random.normal(jax.random.fold_in(_tk, 500 + 14), (1000, 16), jnp.float32)
        tbl_15 = 0.05 * jax.random.normal(jax.random.fold_in(_tk, 500 + 15), (125000, 16), jnp.float32)
        tbl_16 = 0.05 * jax.random.normal(jax.random.fold_in(_tk, 500 + 16), (1250, 16), jnp.float32)
        tbl_17 = 0.05 * jax.random.normal(jax.random.fold_in(_tk, 500 + 17), (1250, 16), jnp.float32)
        tbl_18 = 0.05 * jax.random.normal(jax.random.fold_in(_tk, 500 + 18), (12500, 16), jnp.float32)
        tbl_19 = 0.05 * jax.random.normal(jax.random.fold_in(_tk, 500 + 19), (125000, 16), jnp.float32)
        tbl_20 = 0.05 * jax.random.normal(jax.random.fold_in(_tk, 500 + 20), (12500, 16), jnp.float32)
        tbl_21 = 0.05 * jax.random.normal(jax.random.fold_in(_tk, 500 + 21), (12500, 16), jnp.float32)
        tbl_22 = 0.05 * jax.random.normal(jax.random.fold_in(_tk, 500 + 22), (1250, 16), jnp.float32)
        tbl_23 = 0.05 * jax.random.normal(jax.random.fold_in(_tk, 500 + 23), (1000, 16), jnp.float32)
        tbl_24 = 0.05 * jax.random.normal(jax.random.fold_in(_tk, 500 + 24), (1250, 16), jnp.float32)
        tbl_25 = 0.05 * jax.random.normal(jax.random.fold_in(_tk, 500 + 25), (1000, 16), jnp.float32)
        tbl_26 = 0.05 * jax.random.normal(jax.random.fold_in(_tk, 500 + 26), (1250, 16), jnp.float32)
        tbl_27 = 0.05 * jax.random.normal(jax.random.fold_in(_tk, 500 + 27), (125000, 16), jnp.float32)
        tbl_28 = 0.05 * jax.random.normal(jax.random.fold_in(_tk, 500 + 28), (12500, 16), jnp.float32)
        tbl_29 = 0.05 * jax.random.normal(jax.random.fold_in(_tk, 500 + 29), (1000, 16), jnp.float32)
        tbl_30 = 0.05 * jax.random.normal(jax.random.fold_in(_tk, 500 + 30), (1000, 16), jnp.float32)
        tbl_31 = 0.05 * jax.random.normal(jax.random.fold_in(_tk, 500 + 31), (1000, 16), jnp.float32)
        tbl_32 = 0.05 * jax.random.normal(jax.random.fold_in(_tk, 500 + 32), (12500, 16), jnp.float32)
        tbl_33 = 0.05 * jax.random.normal(jax.random.fold_in(_tk, 500 + 33), (1250, 16), jnp.float32)
        tbl_34 = 0.05 * jax.random.normal(jax.random.fold_in(_tk, 500 + 34), (1250, 16), jnp.float32)
        tbl_35 = 0.05 * jax.random.normal(jax.random.fold_in(_tk, 500 + 35), (125000, 16), jnp.float32)
        tbl_36 = 0.05 * jax.random.normal(jax.random.fold_in(_tk, 500 + 36), (125000, 16), jnp.float32)
        tbl_37 = 0.05 * jax.random.normal(jax.random.fold_in(_tk, 500 + 37), (1250, 16), jnp.float32)
        tbl_38 = 0.05 * jax.random.normal(jax.random.fold_in(_tk, 500 + 38), (1000, 16), jnp.float32)
        _rk = jax.random.fold_in(_tk, 7)
        W_top1 = 0.0606339 * jax.random.normal(jax.random.fold_in(_tk, 801), (272, 512), jnp.float32)
        W_top2 = 0.0441942 * jax.random.normal(jax.random.fold_in(_tk, 802), (512, 256), jnp.float32)
        W_top3 = 0.0625 * jax.random.normal(jax.random.fold_in(_tk, 803), (256, 1), jnp.float32)
        b_top1 = jnp.zeros((512,), jnp.float32)
        b_top2 = jnp.zeros((256,), jnp.float32)
        return (dense_ctx, ids, tbl_0, tbl_1, tbl_2, tbl_3, tbl_4, tbl_5, tbl_6, tbl_7, tbl_8, tbl_9, tbl_10, tbl_11, tbl_12, tbl_13, tbl_14, tbl_15, tbl_16, tbl_17, tbl_18, tbl_19, tbl_20, tbl_21, tbl_22, tbl_23, tbl_24, tbl_25, tbl_26, tbl_27, tbl_28, tbl_29, tbl_30, tbl_31, tbl_32, tbl_33, tbl_34, tbl_35, tbl_36, tbl_37, tbl_38, W_top1, b_top1, W_top2, b_top2, W_top3)
    dense_ctx, ids, tbl_0, tbl_1, tbl_2, tbl_3, tbl_4, tbl_5, tbl_6, tbl_7, tbl_8, tbl_9, tbl_10, tbl_11, tbl_12, tbl_13, tbl_14, tbl_15, tbl_16, tbl_17, tbl_18, tbl_19, tbl_20, tbl_21, tbl_22, tbl_23, tbl_24, tbl_25, tbl_26, tbl_27, tbl_28, tbl_29, tbl_30, tbl_31, tbl_32, tbl_33, tbl_34, tbl_35, tbl_36, tbl_37, tbl_38, W_top1, b_top1, W_top2, b_top2, W_top3 = _rec_inputs()

    def _L0_rec_setup():
        import jax, jax.numpy as jnp
        import numpy as np
        B, F0, D = (256, 39, 16)
        LAYER_SIZES = [128, 128, 128]
        key = jax.random.key(seed)
        ks = jax.random.split(key, 1 + 2 * len(LAYER_SIZES))
        inputs = jax.random.normal(ks[0], (B, F0, D), dtype=jnp.float32)
        out = {'inputs': inputs}
        field_nums = [F0]
        for i, size in enumerate(LAYER_SIZES):
            fk = field_nums[-1]
            fan_in = F0 * fk
            scale = np.sqrt(2.0 / (fan_in + size)).astype(np.float32)
            out[f'w{i}'] = jax.random.normal(ks[1 + 2 * i], (F0, fk, size), dtype=jnp.float32) * scale
            out[f'b{i}'] = jnp.zeros((size,), dtype=jnp.float32)
            field_nums.append(size // 2)
        return out
    _L0_rec_all = _L0_rec_setup()
    _L0_rec_in = {k: v for k, v in _L0_rec_all.items() if k in ('w0', 'w1', 'w2', 'b0', 'b1', 'b2')}
    del _L0_rec_all
    return {'dense_ctx': dense_ctx, 'ids': ids, 'tbl_0': tbl_0, 'tbl_1': tbl_1, 'tbl_2': tbl_2, 'tbl_3': tbl_3, 'tbl_4': tbl_4, 'tbl_5': tbl_5, 'tbl_6': tbl_6, 'tbl_7': tbl_7, 'tbl_8': tbl_8, 'tbl_9': tbl_9, 'tbl_10': tbl_10, 'tbl_11': tbl_11, 'tbl_12': tbl_12, 'tbl_13': tbl_13, 'tbl_14': tbl_14, 'tbl_15': tbl_15, 'tbl_16': tbl_16, 'tbl_17': tbl_17, 'tbl_18': tbl_18, 'tbl_19': tbl_19, 'tbl_20': tbl_20, 'tbl_21': tbl_21, 'tbl_22': tbl_22, 'tbl_23': tbl_23, 'tbl_24': tbl_24, 'tbl_25': tbl_25, 'tbl_26': tbl_26, 'tbl_27': tbl_27, 'tbl_28': tbl_28, 'tbl_29': tbl_29, 'tbl_30': tbl_30, 'tbl_31': tbl_31, 'tbl_32': tbl_32, 'tbl_33': tbl_33, 'tbl_34': tbl_34, 'tbl_35': tbl_35, 'tbl_36': tbl_36, 'tbl_37': tbl_37, 'tbl_38': tbl_38, 'W_top1': W_top1, 'b_top1': b_top1, 'W_top2': W_top2, 'b_top2': b_top2, 'W_top3': W_top3, 'L0_rec_w0': _L0_rec_in['w0'], 'L0_rec_w1': _L0_rec_in['w1'], 'L0_rec_w2': _L0_rec_in['w2'], 'L0_rec_b0': _L0_rec_in['b0'], 'L0_rec_b1': _L0_rec_in['b1'], 'L0_rec_b2': _L0_rec_in['b2']}

def reference(dense_ctx, ids, tbl_0, tbl_1, tbl_2, tbl_3, tbl_4, tbl_5, tbl_6, tbl_7, tbl_8, tbl_9, tbl_10, tbl_11, tbl_12, tbl_13, tbl_14, tbl_15, tbl_16, tbl_17, tbl_18, tbl_19, tbl_20, tbl_21, tbl_22, tbl_23, tbl_24, tbl_25, tbl_26, tbl_27, tbl_28, tbl_29, tbl_30, tbl_31, tbl_32, tbl_33, tbl_34, tbl_35, tbl_36, tbl_37, tbl_38, W_top1, b_top1, W_top2, b_top2, W_top3, L0_rec_w0, L0_rec_w1, L0_rec_w2, L0_rec_b0, L0_rec_b1, L0_rec_b2):
    import jax
    import jax.numpy as jnp

    def _L0_rec_ref(inputs, w0, w1, w2, b0, b1, b2):
        import jax, jax.numpy as jnp
        import numpy as np
        B, F0, D = (256, 39, 16)
        LAYER_SIZES = [128, 128, 128]
        x0 = inputs
        xk = inputs
        params = [(w0, b0), (w1, b1), (w2, b2)]
        n_layers = len(params)
        direct = []
        for idx, (W, b) in enumerate(params):
            z = jnp.einsum('bhd,bkd,hks->bsd', x0, xk, W) + b[None, :, None]
            z = jax.nn.relu(z)
            if idx != n_layers - 1:
                half = z.shape[1] // 2
                xk = z[:, :half, :]
                direct.append(z[:, half:, :])
            else:
                direct.append(z)
        logit = jnp.sum(jnp.concatenate(direct, axis=1), axis=-1)
        return logit
    e = jnp.stack([tbl_0[ids[:, 0]], tbl_1[ids[:, 1]], tbl_2[ids[:, 2]], tbl_3[ids[:, 3]], tbl_4[ids[:, 4]], tbl_5[ids[:, 5]], tbl_6[ids[:, 6]], tbl_7[ids[:, 7]], tbl_8[ids[:, 8]], tbl_9[ids[:, 9]], tbl_10[ids[:, 10]], tbl_11[ids[:, 11]], tbl_12[ids[:, 12]], tbl_13[ids[:, 13]], tbl_14[ids[:, 14]], tbl_15[ids[:, 15]], tbl_16[ids[:, 16]], tbl_17[ids[:, 17]], tbl_18[ids[:, 18]], tbl_19[ids[:, 19]], tbl_20[ids[:, 20]], tbl_21[ids[:, 21]], tbl_22[ids[:, 22]], tbl_23[ids[:, 23]], tbl_24[ids[:, 24]], tbl_25[ids[:, 25]], tbl_26[ids[:, 26]], tbl_27[ids[:, 27]], tbl_28[ids[:, 28]], tbl_29[ids[:, 29]], tbl_30[ids[:, 30]], tbl_31[ids[:, 31]], tbl_32[ids[:, 32]], tbl_33[ids[:, 33]], tbl_34[ids[:, 34]], tbl_35[ids[:, 35]], tbl_36[ids[:, 36]], tbl_37[ids[:, 37]], tbl_38[ids[:, 38]]], axis=1)
    z = _L0_rec_ref(e, L0_rec_w0, L0_rec_w1, L0_rec_w2, L0_rec_b0, L0_rec_b1, L0_rec_b2)
    z = z.reshape(z.shape[0], -1)
    h = jnp.concatenate([z, dense_ctx], axis=1)
    h = jnp.maximum(h @ W_top1 + b_top1, 0.0)
    h = jnp.maximum(h @ W_top2 + b_top2, 0.0)
    y = h @ W_top3
    return y

_drawn_inputs = setup_inputs


def setup_inputs(seed=0):
    import zlib

    import numpy as np

    out = dict(_drawn_inputs(seed))
    spreads = {'b_top1': (0.0, 2.0),
     'b_top2': (0.0, 2.0),
     'L0_rec_b0': (0.0, 0.34),
     'L0_rec_b1': (0.0, 0.535),
     'L0_rec_b2': (0.0, 0.8)}
    factors = {'tbl_0': 8.0,
     'tbl_1': 8.0,
     'tbl_2': 8.0,
     'tbl_3': 8.0,
     'tbl_4': 8.0,
     'tbl_5': 8.0,
     'tbl_6': 8.0,
     'tbl_7': 8.0,
     'tbl_8': 8.0,
     'tbl_9': 8.0,
     'tbl_10': 8.0,
     'tbl_11': 8.0,
     'tbl_12': 8.0,
     'tbl_13': 8.0,
     'tbl_14': 8.0,
     'tbl_15': 8.0,
     'tbl_16': 8.0,
     'tbl_17': 8.0,
     'tbl_18': 8.0,
     'tbl_19': 8.0,
     'tbl_20': 8.0,
     'tbl_21': 8.0,
     'tbl_22': 8.0,
     'tbl_23': 8.0,
     'tbl_24': 8.0,
     'tbl_25': 8.0,
     'tbl_26': 8.0,
     'tbl_27': 8.0,
     'tbl_28': 8.0,
     'tbl_29': 8.0,
     'tbl_30': 8.0,
     'tbl_31': 8.0,
     'tbl_32': 8.0,
     'tbl_33': 8.0,
     'tbl_34': 8.0,
     'tbl_35': 8.0,
     'tbl_36': 8.0,
     'tbl_37': 8.0,
     'tbl_38': 8.0,
     'L0_rec_w0': 8.0,
     'L0_rec_w1': 6.24,
     'L0_rec_w2': 4.552,
     'dense_ctx': 8.0}
    for name, (base, spread) in spreads.items():
        noise = np.random.default_rng([zlib.crc32(name.encode()), seed]).standard_normal(out[name].shape)
        drawn = base * np.exp(spread * noise) if base else spread * noise
        out[name] = jnp.asarray(drawn.astype(out[name].dtype))
    for name, factor in factors.items():
        out[name] = (out[name] * factor).astype(out[name].dtype)
    return out
```

```python
from contextlib import ExitStack

import concourse.bass as bass
from concourse import mybir

F32 = mybir.dt.float32
I32 = mybir.dt.int32
ALU = mybir.AluOpType
ACT = mybir.ActivationFunctionType
AX_X = mybir.AxisListType.X

P = 128
FIELDS = 39
DIM = 16
BATCH = 1024
SIZE = 128
HALF = SIZE // 2
TILE = 1024
SAMPLES = TILE // DIM
TILES = BATCH // SAMPLES
BANK = 512
NB = TILE // BANK

GROUPS = P // FIELDS
GP = GROUPS * FIELDS
SLOTS = -(-SAMPLES // GROUPS)
LAST_SLOTS = SAMPLES - (GROUPS - 1) * SLOTS

ROTATIONS = FIELDS // 2 + 1
C0 = -(-ROTATIONS // GROUPS)
C0_ROWS = [FIELDS * min(GROUPS, ROTATIONS - GROUPS * c) for c in range(C0)]
C1 = -(-FIELDS // 2)
C1_ROWS = [HALF * min(2, FIELDS - 2 * c) for c in range(C1)]
PAIR = 2
PAIRS0 = -(-C0 // PAIR)
PAIRS1 = -(-C1 // PAIR)
PAIRS_TILE = PAIRS0 + 2 * PAIRS1
RING = 3
SPREAD = 4
SPREADS = -(-C1 // SPREAD)
PREP = PAIRS0 + PAIRS1
assert PAIRS_TILE % RING == 0

H1 = 512
H2 = 256
CTX = 16
M1 = H1 // P
M2 = H2 // P
NH = BATCH // BANK


def tower(nc, table, ids, offsets, ctx_t, w0a, w0b, w1, w2, b0, b1, b2, wt1, bt1, wt2, bt2, wt3, out):
    with ExitStack() as ctx:
        def sb(name, shape, dt=F32):
            return ctx.enter_context(nc.sbuf_tensor(name, shape, dt))

        def sem(name):
            return ctx.enter_context(nc.semaphore(name))

        x0_dram = nc.dram_tensor("x0_rows", [TILES, 2 * FIELDS, TILE], F32, kind="Internal").ap()

        ids_sb = sb("ids_sb", [GP, TILES * SLOTS], I32)
        offsets_sb = sb("offsets_sb", [GP, SLOTS], I32)
        rows_sb = sb("rows_sb", [GP, SLOTS], I32)
        gathered = sb("gathered", [GP, SLOTS * DIM])
        x0_rep = sb("x0_rep", [GP, TILE])
        x0_rot = sb("x0_rot", [GP, C0, TILE])
        x0_spread = sb("x0_spread", [P, C1, TILE])
        prod = sb("prod", [P, RING, PAIR, TILE])
        x1 = sb("x1", [P, TILE])
        x2 = sb("x2", [P, TILE])
        direct01 = sb("direct01", [P, TILE])
        direct2 = sb("direct2", [P, TILE])
        w0_sb = sb("w0_sb", [GP, C0, SIZE])
        w0b_sb = sb("w0b_sb", [GP, C0, SIZE])
        w1_sb = sb("w1_sb", [P, C1, SIZE])
        w2_sb = sb("w2_sb", [P, C1, SIZE])
        b0_sb = sb("b0_sb", [P, 1])
        b1_sb = sb("b1_sb", [P, 1])
        b2_sb = sb("b2_sb", [P, 1])
        z = sb("z", [P, 2, BATCH])
        ctx_sb = sb("ctx_sb", [CTX, BATCH])
        wt1_sb = sb("wt1_sb", [P, 2, H1])
        wt1c_sb = sb("wt1c_sb", [CTX, H1])
        wt2_sb = sb("wt2_sb", [P, M1, H2])
        wt3_sb = sb("wt3_sb", [P, M2])
        bt1_sb = sb("bt1_sb", [P, M1])
        bt2_sb = sb("bt2_sb", [P, M2])
        h1 = x0_spread[:, 0:M1, :]
        h2 = x0_spread[:, M1:M1 + M2, :]
        y = x0_spread[0:1, M1 + M2, :]

        ps = ctx.enter_context(nc.psum_tensor("ps", [P, 8, BANK], F32))
        ps0, ps1, ps2 = (ps[:, NB * i:NB * i + NB, :] for i in range(3))

        ids_loaded = sem("ids_loaded")
        rows_ready = sem("rows_ready")
        rows_seen = sem("rows_seen")
        tile_gathered = sem("tile_gathered")
        x0_written = sem("x0_written")
        rep_loaded = sem("rep_loaded")
        rot_loaded = sem("rot_loaded")
        spread_loaded = [sem(f"spread_loaded{i}") for i in range(SPREADS)]
        w0_zeroed = sem("w0_zeroed")
        w0_loaded = sem("w0_loaded")
        w0_ready = sem("w0_ready")
        w1_loaded = sem("w1_loaded")
        w2_loaded = sem("w2_loaded")
        biases_loaded = sem("biases_loaded")
        top_loaded = sem("top_loaded")
        prod_ready = sem("prod_ready")
        prod_used = sem("prod_used")
        x1_ready = sem("x1_ready")
        x2_ready = sem("x2_ready")
        direct0_ready = sem("direct0_ready")
        direct1_ready = sem("direct1_ready")
        direct2_ready = sem("direct2_ready")
        sum01_done = sem("sum01_done")
        sum2_done = sem("sum2_done")
        h1_done = sem("h1_done")
        h1_ready = sem("h1_ready")
        h2_done = sem("h2_done")
        h2_ready = sem("h2_ready")
        y_done = sem("y_done")
        y_ready = sem("y_ready")
        out_written = sem("out_written")

        def end0(tile):
            return PREP + (tile - 1) * PAIRS_TILE + PAIRS0

        def end1(tile):
            return PREP + tile * PAIRS_TILE

        def end2(tile):
            return end0(tile + 1) + PAIRS1

        block = ctx.enter_context(nc.Block())

        @block.gpsimd
        def _(pool):
            pool.wait_ge(ids_loaded, 32)

            def gather_tile(t):
                nc.gpsimd.tensor_tensor(rows_sb[:], ids_sb[:, bass.ds(t * SLOTS, SLOTS)], offsets_sb[:],
                                        ALU.add).then_inc(rows_ready, 1)
                pool.wait_ge(rows_ready, t + 1)
                pool.sem_inc(rows_seen, 1)
                for j in range(SLOTS):
                    nc.gpsimd.indirect_dma_start(
                        gathered[:, DIM * j:DIM * (j + 1)], None, table[:, :],
                        bass.IndirectOffsetOnAxis(ap=rows_sb[:, j:j + 1], axis=0),
                    ).then_inc(tile_gathered, 16)
                pool.wait_ge(tile_gathered, 16 * SLOTS * (t + 1))
                for r in range(GROUPS):
                    n = DIM * (SLOTS if r < GROUPS - 1 else LAST_SLOTS)
                    src = gathered[FIELDS * r:FIELDS * (r + 1), 0:n]
                    for twice in range(2):
                        dst = bass.AP(tensor=x0_dram.tensor,
                                      offset=t * (2 * FIELDS * TILE) + (twice * FIELDS * TILE + r * SLOTS * DIM),
                                      ap=[[TILE, FIELDS], [1, n]])
                        pool.dma_start(dst, src).then_inc(x0_written, 16)
                pool.wait_ge(x0_written, 16 * 2 * GROUPS * (t + 1))

            with pool.Fori(0, TILES) as t:
                gather_tile(t)

        @block.sync
        def _(sp):
            sp.dma_start(ids_sb[:], ids).then_inc(ids_loaded, 16)
            sp.dma_start(offsets_sb[:], offsets).then_inc(ids_loaded, 16)
            for g in range(GROUPS):
                n = -(-(ROTATIONS - g) // GROUPS)
                rows = slice(FIELDS * g, FIELDS * (g + 1))
                sp.dma_start(w0_sb[rows, 0:n, :], w0a[g::GROUPS].rearrange("c i s -> i c s")).then_inc(w0_loaded, 16)
            sp.wait_ge(w0_zeroed, 1)
            for g in range(GROUPS):
                n = -(-(ROTATIONS - g) // GROUPS)
                rows = slice(FIELDS * g, FIELDS * (g + 1))
                first = 1 if g == 0 else 0
                sp.dma_start(w0b_sb[rows, first:n, :],
                             w0b[g + GROUPS * first::GROUPS].rearrange("c i s -> i c s")).then_inc(w0_loaded, 16)

            def x0_rows(t, first, pattern):
                return bass.AP(tensor=x0_dram.tensor, offset=t * (2 * FIELDS * TILE) + first * TILE, ap=pattern)

            def load_rotations(t):
                sp.wait_ge(x0_written, 16 * 2 * GROUPS * (t + 1))
                for g in range(GROUPS):
                    rows = slice(FIELDS * g, FIELDS * (g + 1))
                    n = -(-(ROTATIONS - g) // GROUPS)
                    sp.dma_start(x0_rep[rows, :], x0_rows(t, 0, [[TILE, FIELDS], [1, TILE]])).then_inc(rep_loaded, 16)
                    sp.dma_start(x0_rot[rows, 0:n, :],
                                 x0_rows(t, g, [[TILE, FIELDS], [GROUPS * TILE, n], [1, TILE]])).then_inc(rot_loaded, 16)

            def load_spread(t, i):
                c = SPREAD * i
                for g in range(2):
                    n = min(SPREAD, (FIELDS - g + 1) // 2 - c)
                    sp.dma_start(x0_spread[HALF * g:HALF * (g + 1), c:c + n, :],
                                 x0_rows(t, 2 * c + g, [[0, HALF], [2 * TILE, n], [1, TILE]])
                                 ).then_inc(spread_loaded[i], 16)

            load_rotations(0)
            for i in range(SPREADS):
                load_spread(0, i)
                if i == 0:
                    sp.dma_start(w1_sb[:, 0:C1 - 1, :],
                                 w1[0:(C1 - 1) * P, :].rearrange("(c p) s -> p c s", p=P)).then_inc(w1_loaded, 16)
                    sp.dma_start(w1_sb[0:HALF, C1 - 1, :], w1[(C1 - 1) * P:, :]).then_inc(w1_loaded, 16)
                    for b, b_sb in ((b0, b0_sb), (b1, b1_sb), (b2, b2_sb)):
                        sp.dma_start(b_sb[:], b.rearrange("(s a) -> s a", a=1)).then_inc(biases_loaded, 16)
            sp.dma_start(w2_sb[:, 0:C1 - 1, :],
                         w2[0:(C1 - 1) * P, :].rearrange("(c p) s -> p c s", p=P)).then_inc(w2_loaded, 16)
            sp.dma_start(w2_sb[0:HALF, C1 - 1, :], w2[(C1 - 1) * P:, :]).then_inc(w2_loaded, 16)
            for dst, src in ((ctx_sb[:], ctx_t),
                             (wt1_sb[:], wt1[0:2 * P, :].rearrange("(c p) n -> p c n", p=P)),
                             (wt1c_sb[:], wt1[2 * P:, :]),
                             (wt2_sb[:], wt2.rearrange("(c p) n -> p c n", p=P)),
                             (wt3_sb[:], wt3), (bt1_sb[:], bt1), (bt2_sb[:], bt2)):
                sp.dma_start(dst, src).then_inc(top_loaded, 16)

            with sp.Fori(0, TILES - 1) as t:
                sp.wait_ge(prod_ready, end1(t) - PAIRS1)
                load_rotations(t + 1)
                for i in range(SPREADS):
                    sp.wait_ge(prod_ready, end0(t + 1) + min(SPREAD // PAIR * (i + 1), PAIRS1))
                    load_spread(t + 1, i)

            sp.wait_ge(y_ready, NH)
            sp.dma_start(out.rearrange("b a -> a b"), y).then_inc(out_written, 16)
            sp.wait_ge(out_written, 16)

        @block.vector
        def _(dve):
            dve.sem_inc(sum01_done, 1)
            dve.sem_inc(sum2_done, 1)
            nc.vector.memset(w0b_sb[:, 0, :], 0.0).then_inc(w0_zeroed, 1)
            dve.wait_ge(w0_loaded, 16 * 2 * GROUPS)
            nc.vector.tensor_tensor(w0_sb[:, 0:C0 - 1, :], w0_sb[:, 0:C0 - 1, :], w0b_sb[:, 0:C0 - 1, :],
                                    ALU.add).then_inc(w0_ready, 1)
            rows = C0_ROWS[C0 - 1]
            nc.vector.tensor_tensor(w0_sb[0:rows, C0 - 1, :], w0_sb[0:rows, C0 - 1, :], w0b_sb[0:rows, C0 - 1, :],
                                    ALU.add).then_inc(w0_ready, 1)

            def runs(chunk_rows, pair):
                cs = list(range(PAIR * pair, min(PAIR * pair + PAIR, len(chunk_rows))))
                if len({chunk_rows[c] for c in cs}) == 1:
                    return [(0, cs[0], len(cs), chunk_rows[cs[0]])]
                return [(k, c, 1, chunk_rows[c]) for k, c in enumerate(cs)]

            def products(slot, pair, chunk_rows, left, right):
                for k, c, n, rows in runs(chunk_rows, pair):
                    last = nc.vector.tensor_tensor(prod[0:rows, slot, k:k + n, :], left(rows, c, n),
                                                   right(rows, c, n), ALU.mult)
                last.then_inc(prod_ready, 1)

            def same(x):
                return lambda rows, c, n: x[0:rows, :].unsqueeze(1).to_broadcast([rows, n, TILE])

            def chunks_of(x):
                return lambda rows, c, n: x[0:rows, c:c + n, :]

            def layer0(t, at, count):
                dve.wait_ge(rep_loaded, 16 * GROUPS * (t + 1))
                dve.wait_ge(rot_loaded, 16 * GROUPS * (t + 1))
                for q in range(PAIRS0):
                    if at + q >= RING:
                        dve.wait_ge(prod_used, count + (q + 1 - RING))
                    products((at + q) % RING, q, C0_ROWS, same(x0_rep), chunks_of(x0_rot))

            def layer12(t, at, count, x, after):
                for q in range(PAIRS1):
                    if x is x1 and PAIR * q % SPREAD == 0:
                        dve.wait_ge(spread_loaded[PAIR * q // SPREAD], 32 * (t + 1))
                    if at + q >= RING:
                        dve.wait_ge(prod_used, count + (q + 1 - RING))
                    products((at + q) % RING, q, C1_ROWS, chunks_of(x0_spread), same(x))
                    if q == 1:
                        after()

            def sum_dims(z_out, src):
                return nc.vector.tensor_reduce(z_out, src.rearrange("p (b d) -> p b d", d=DIM), AX_X, ALU.add)

            def sum01(t):
                dve.wait_ge(direct0_ready, t + 1)
                dve.wait_ge(direct1_ready, t + 1)
                sum_dims(z[:, 0, bass.ds(t * SAMPLES, SAMPLES)], direct01[:, :]).then_inc(sum01_done, 1)

            def sum2(t):
                dve.wait_ge(direct2_ready, t + 2)
                sum_dims(z[:, 1, bass.ds(t * SAMPLES, SAMPLES)], direct2[:, :]).then_inc(sum2_done, 1)

            layer0(0, 0, 0)
            dve.wait_ge(x1_ready, 2)
            layer12(0, PAIRS0, PAIRS0, x1, lambda: None)
            with dve.Fori(0, TILES - 1) as t:
                at = PREP
                layer0(t + 1, at, t * PAIRS_TILE + at)
                dve.wait_ge(x2_ready, 2 * (t + 1))
                at += PAIRS0
                layer12(t, at, t * PAIRS_TILE + at, x2, lambda: sum01(t))
                dve.wait_ge(x1_ready, 2 * (t + 2))
                at += PAIRS1
                layer12(t + 1, at, t * PAIRS_TILE + at, x1, lambda: sum2(t))
            last = TILES - 1
            dve.wait_ge(x2_ready, 2 * TILES)
            layer12(last, PREP + last * PAIRS_TILE, PREP + last * PAIRS_TILE, x2, lambda: sum01(last))
            sum2(last)
            for n in range(NH):
                dve.wait_ge(y_done, n + 1)
                nc.vector.tensor_copy(y[:, BANK * n:BANK * (n + 1)], ps[0:1, n, :]).then_inc(y_ready, 1)

        @block.tensor
        def _(pe):
            def layer(at, count, chunk_rows, w, out_ps):
                for q in range(-(-len(chunk_rows) // PAIR)):
                    pe.wait_ge(prod_ready, count + (q + 1))
                    for k in range(PAIR):
                        c = PAIR * q + k
                        if c >= len(chunk_rows):
                            continue
                        rows = chunk_rows[c]
                        for n in range(NB):
                            mm = nc.tensor.matmul(out_ps[:, n, :], w[0:rows, c, :],
                                                  prod[0:rows, (at + q) % RING, k, BANK * n:BANK * (n + 1)],
                                                  start=(c == 0), stop=(c == len(chunk_rows) - 1))
                    mm.then_inc(prod_used, 1)

            pe.wait_ge(w0_ready, 2)
            layer(0, 0, C0_ROWS, w0_sb, ps0)
            pe.wait_ge(w1_loaded, 32)
            layer(PAIRS0, PAIRS0, C1_ROWS, w1_sb, ps1)
            pe.wait_ge(w2_loaded, 32)
            with pe.Fori(0, TILES - 1) as t:
                at = PREP
                pe.wait_ge(direct0_ready, t + 1)
                layer(at, t * PAIRS_TILE + at, C0_ROWS, w0_sb, ps0)
                at += PAIRS0
                pe.wait_ge(direct2_ready, t + 1)
                layer(at, t * PAIRS_TILE + at, C1_ROWS, w2_sb, ps2)
                at += PAIRS1
                pe.wait_ge(direct1_ready, t + 1)
                layer(at, t * PAIRS_TILE + at, C1_ROWS, w1_sb, ps1)
            pe.wait_ge(direct2_ready, TILES)
            at = PREP + (TILES - 1) * PAIRS_TILE
            layer(at, at, C1_ROWS, w2_sb, ps2)

            pe.wait_ge(top_loaded, 16 * 7)
            pe.wait_ge(direct2_ready, TILES + 1)
            pe.wait_ge(sum01_done, TILES + 1)
            pe.wait_ge(sum2_done, TILES + 1)
            for n in range(NH):
                cols = slice(BANK * n, BANK * (n + 1))
                for m in range(M1):
                    outs = slice(P * m, P * (m + 1))
                    nc.tensor.matmul(ps[:, M1 * n + m, :], wt1_sb[:, 0, outs], z[:, 0, cols], start=True, stop=False)
                    nc.tensor.matmul(ps[:, M1 * n + m, :], wt1_sb[:, 1, outs], z[:, 1, cols], start=False, stop=False)
                    nc.tensor.matmul(ps[:, M1 * n + m, :], wt1c_sb[:, outs], ctx_sb[:, cols],
                                     start=False, stop=True).then_inc(h1_done, 1)
            for n in range(NH):
                for m in range(M2):
                    pe.wait_ge(h1_ready, M1 * (n + 1))
                    for c in range(M1):
                        mm = nc.tensor.matmul(ps[:, M1 * n + m, :], wt2_sb[:, c, P * m:P * (m + 1)],
                                              h1[:, c, BANK * n:BANK * (n + 1)], start=(c == 0), stop=(c == M1 - 1))
                    mm.then_inc(h2_done, 1)
            for n in range(NH):
                pe.wait_ge(h2_ready, M2 * (n + 1))
                for c in range(M2):
                    mm = nc.tensor.matmul(ps[0:1, n, :], wt3_sb[:, c:c + 1], h2[:, c, BANK * n:BANK * (n + 1)],
                                          start=(c == 0), stop=(c == M2 - 1))
                mm.then_inc(y_done, 1)

        @block.scalar
        def _(act):
            def relu(dst, src, bias):
                return nc.scalar.activation(dst, src, ACT.Relu, bias=bias)

            def flat(out_ps, rows):
                return out_ps[rows, :, :].rearrange("p n c -> p (n c)")

            LOW, HIGH = slice(0, HALF), slice(HALF, SIZE)

            def split_outputs(t, end, out_ps, bias, x, x_ready, direct, direct_ready):
                act.wait_ge(prod_used, end)
                for half in (LOW, HIGH):
                    relu(x[half, :], flat(out_ps, LOW), bias[LOW, :]).then_inc(x_ready, 1)
                act.wait_ge(sum01_done, t + 1)
                relu(direct, flat(out_ps, HIGH), bias[HIGH, :]).then_inc(direct_ready, 1)

            def outputs0(t, end):
                split_outputs(t, end, ps0, b0_sb, x1, x1_ready, direct01[LOW, :], direct0_ready)

            def outputs1(t):
                split_outputs(t, end1(t), ps1, b1_sb, x2, x2_ready, direct01[HIGH, :], direct1_ready)

            def outputs2(t, end):
                act.wait_ge(prod_used, end)
                act.wait_ge(sum2_done, t + 1)
                relu(direct2[:, :], flat(ps2, slice(0, P)), b2_sb[:, :]).then_inc(direct2_ready, 1)

            act.sem_inc(direct2_ready, 1)
            act.wait_ge(biases_loaded, 16 * 3)
            outputs0(0, PAIRS0)
            outputs1(0)
            with act.Fori(0, TILES - 1) as t:
                outputs0(t + 1, end0(t + 1))
                outputs2(t, end2(t))
                outputs1(t + 1)
            outputs2(TILES - 1, end1(TILES - 1) + PAIRS1)

            act.wait_ge(top_loaded, 16 * 7)
            for n in range(NH):
                for m in range(M1):
                    act.wait_ge(h1_done, M1 * n + m + 1)
                    relu(h1[:, m, BANK * n:BANK * (n + 1)], ps[:, M1 * n + m, :], bt1_sb[:, m:m + 1]).then_inc(h1_ready, 1)
            for n in range(NH):
                for m in range(M2):
                    act.wait_ge(h2_done, M2 * n + m + 1)
                    relu(h2[:, m, BANK * n:BANK * (n + 1)], ps[:, M1 * n + m, :], bt2_sb[:, m:m + 1]).then_inc(h2_ready, 1)


def kernel(**inputs):
    import numpy as np
    import concourse.bacc as bacc
    from concourse.bass_utils import run_bass_kernel_spmd

    a = {k: np.asarray(v) for k, v in inputs.items()}
    tables = [a[f"tbl_{f}"] for f in range(FIELDS)]
    starts = np.cumsum([0] + [t.shape[0] for t in tables[:-1]]).astype(np.int32)

    sample = np.minimum(np.arange(GROUPS)[:, None] * SLOTS + np.arange(SLOTS)[None, :], SAMPLES - 1)
    ids = a["ids"].reshape(TILES, SAMPLES, FIELDS)[:, sample, :]
    ids = ids.transpose(1, 3, 0, 2).reshape(GP, TILES * SLOTS)
    offsets = np.broadcast_to(np.tile(starts, GROUPS)[:, None], (GP, SLOTS))

    i = np.arange(FIELDS)[None, :]
    k = (i + np.arange(ROTATIONS)[:, None]) % FIELDS
    w0 = a["L0_rec_w0"]
    host = {
        "table": np.concatenate(tables, axis=0),
        "ids": ids, "offsets": offsets,
        "ctx_t": a["dense_ctx"].T,
        "w0a": w0[i, k], "w0b": w0[k, i],
        "w1": a["L0_rec_w1"].reshape(FIELDS * HALF, SIZE),
        "w2": a["L0_rec_w2"].reshape(FIELDS * HALF, SIZE),
        "b0": a["L0_rec_b0"], "b1": a["L0_rec_b1"], "b2": a["L0_rec_b2"],
        "wt1": a["W_top1"], "bt1": a["b_top1"].reshape(M1, P).T,
        "wt2": a["W_top2"], "bt2": a["b_top2"].reshape(M2, P).T,
        "wt3": a["W_top3"].reshape(M2, P).T,
    }
    host = {k_: np.ascontiguousarray(v) for k_, v in host.items()}
    nc = bacc.Bacc("TRN2", target_bir_lowering=False, num_devices=1)
    args = [nc.dram_tensor(k_, v.shape, mybir.dt.from_np(v.dtype), kind="ExternalInput").ap() for k_, v in host.items()]
    args.append(nc.dram_tensor("out", (BATCH, 1), F32, kind="ExternalOutput").ap())
    tower(nc, *args)
    result = run_bass_kernel_spmd(nc, [host], core_ids=[0])
    return result.results[0]["out"]
```

```python
from contextlib import ExitStack

import concourse.bass as bass
from concourse import mybir

F32 = mybir.dt.float32
F32R = mybir.dt.float32r
I32 = mybir.dt.int32
ALU = mybir.AluOpType
ACT = mybir.ActivationFunctionType
AX_X = mybir.AxisListType.X

P = 128
FIELDS = 39
DIM = 16
BATCH = 1024
SIZE = 128
HALF = SIZE // 2
TILE = 512
SAMPLES = TILE // DIM
TILES = BATCH // SAMPLES

GROUPS = P // FIELDS
GP = GROUPS * FIELDS
SLOTS = -(-SAMPLES // GROUPS)
LAST_SLOTS = SAMPLES - (GROUPS - 1) * SLOTS

ROTATIONS = FIELDS // 2 + 1
C0 = -(-ROTATIONS // GROUPS)
C0_ROWS = [FIELDS * min(GROUPS, ROTATIONS - GROUPS * c) for c in range(C0)]
C1 = -(-FIELDS // 2)
C1_ROWS = [P] * C1
UNIT = 4

NATIVE, OWN, POOL, STACKED = range(4)
UNITS = {
    "0a": (OWN, 0, 3), "0b": (NATIVE, 3, C0),
    "1a": (NATIVE, 12, 16), "1b": (POOL, 0, 4), "1c": (OWN, 8, 12), "1d": (POOL, 4, 8),
    "1e": (NATIVE, 16, C1 - 1), "1s": (STACKED, C1 - 1, C1),
    "2a": (NATIVE, 12, 16), "2b": (POOL, 0, 4), "2c": (NATIVE, 8, 12), "2d": (POOL, 4, 8),
    "2e": (NATIVE, 16, C1 - 1), "2s": (STACKED, C1 - 1, C1),
}
SPLIT = [3, 12, 8]
SPREAD = {u[1]: UNITS[u][1:] for u in ("1a", "1b", "1c", "1d")}
SPREAD["e"] = (16, C1)

START, END = "start", "end"
FORMED = (["0a", "0b", "1a", "1b", "1c", "1d", "1e"],
          ["0a", "0b", "2a", "2b", "2c", "2d", "1a", "1b", "2e", "1c", "1d", "1e"],
          ["2a", "2b", "2c", "2d", "2e"])
HIGHS = (["0a", "1b", "1c", "1d", "1s"],
         ["0a", "2b", "2d", "1b", "2s", "1c", "1d", "1s"],
         ["2b", "2d", "2s"])
OWN_LOWS = (["0a", "1c", "1s"],
            ["0a", "2s", "1c", "1s"],
            ["2s"])
POOL_LOWS = (["1b", "1d"],
             ["2b", "2d", "1b", "1d"],
             ["2b", "2d"])
TAKEN = (["0b", "0a", "1a", "1b", "1c", "1e", "1d", "1s"],
         ["0b", "0a", "2a", "2c", "2b", "1a", "2d", "2e", "2s", "1b", "1c", "1e", "1d", "1s"],
         ["2a", "2c", "2b", "2d", "2e", "2s"])
RING = 4
POOL_RING = 2


def count(steps, t, unit=None, kinds=range(4), ago=0):
    start, turn, end = steps

    def of_kinds(units):
        return sum(UNITS[u][0] in kinds for u in units)

    def upto(units):
        return of_kinds(units[:units.index(unit) + 1]) if unit else 0

    if t is START:
        return upto(start)
    if t is END:
        return of_kinds(start) + of_kinds(turn) * (TILES - 1 - ago) + upto(turn if ago else end)
    return of_kinds(start) + upto(turn) - of_kinds(turn) * ago + t * of_kinds(turn)


def slot(t, unit):
    return (count(FORMED, t if t is START or t is END else 0, unit) - 1) % RING


assert len(FORMED[1]) % RING == 0
assert [UNITS[u][0] for u in FORMED[0][1 - RING:]] == [UNITS[u][0] for u in FORMED[1][1 - RING:]]


H1 = 512
H2 = 256
CTX = 16
M1 = H1 // P
M2 = H2 // P
BANK = 512
NH = BATCH // BANK


def tower(nc, table, ids, offsets, ctx_t, w0a, w0b, w1, w2, b0, b1, b2, wt1, bt1, wt2, bt2, wt3, out):
    with ExitStack() as ctx:
        def sb(name, shape, dt=F32):
            return ctx.enter_context(nc.sbuf_tensor(name, shape, dt))

        def sem(name):
            return ctx.enter_context(nc.semaphore(name))

        x0_dram = nc.dram_tensor("x0_rows", [TILES, 2 * FIELDS, TILE], F32, kind="Internal").ap()

        ids_sb = sb("ids_sb", [GP, TILES * SLOTS], I32)
        offsets_sb = sb("offsets_sb", [GP, SLOTS], I32)
        rows_sb = sb("rows_sb", [GP, SLOTS], I32)
        gathered = sb("gathered", [GP, SLOTS * DIM])
        leaving = sb("leaving", [GP, SLOTS * DIM])
        x0_rep = sb("x0_rep", [GP, TILE])
        x0_rot = sb("x0_rot", [GP, C0, TILE])
        x0_spread = sb("x0_spread", [P, C1, TILE])
        prod = sb("prod", [P, RING, UNIT, TILE])
        own_hi = sb("own_hi", [P, UNIT, TILE], F32R)
        own_lo = sb("own_lo", [P, UNIT, TILE], F32R)
        pool_hi = sb("pool_hi", [P, POOL_RING, UNIT, TILE], F32R)
        pool_lo = sb("pool_lo", [P, POOL_RING, UNIT, TILE], F32R)
        stacked = sb("stacked", [P, TILE], F32R)
        direct01 = sb("direct01", [P, TILE])
        direct2 = sb("direct2", [P, TILE])
        w0_sb = sb("w0_sb", [GP, C0, SIZE])
        w1_sb = sb("w1_sb", [P, C1 - 1 - SPLIT[1], SIZE])
        w2_sb = sb("w2_sb", [P, C1 - 1 - SPLIT[2], SIZE])
        w0_hi = sb("w0_hi", [GP, SPLIT[0], SIZE], F32R)
        w0_lo = sb("w0_lo", [GP, SPLIT[0], SIZE], F32R)
        w1_hi = sb("w1_hi", [P, SPLIT[1], SIZE], F32R)
        w1_lo = sb("w1_lo", [P, SPLIT[1], SIZE], F32R)
        w2_hi = sb("w2_hi", [P, SPLIT[2], SIZE], F32R)
        w2_lo = sb("w2_lo", [P, SPLIT[2], SIZE], F32R)
        ws_hi = sb("ws_hi", [P, 2, SIZE], F32R)
        ws_lo = sb("ws_lo", [HALF, 2, SIZE], F32R)
        b0_sb = sb("b0_sb", [P, 1])
        b1_sb = sb("b1_sb", [P, 1])
        b2_sb = sb("b2_sb", [P, 1])
        z = sb("z", [P, 2, BATCH])
        ctx_sb = sb("ctx_sb", [CTX, BATCH])
        wt1_sb = sb("wt1_sb", [P, 2, H1])
        wt1c_sb = sb("wt1c_sb", [CTX, H1])
        wt2_sb = sb("wt2_sb", [P, M1, H2])
        wt3_sb = sb("wt3_sb", [P, M2])
        bt1_sb = sb("bt1_sb", [P, M1])
        bt2_sb = sb("bt2_sb", [P, M2])

        def staged(slot, rows, chunks):
            return prod[0:rows, slot, :, :].rearrange("p u n -> p (u n)")[:, 0:chunks * SIZE].rearrange(
                "p (c s) -> p c s", s=SIZE)

        w1_staged, w2_staged, w0b_staged = staged(0, P, SPLIT[1]), staged(1, P, SPLIT[2]), staged(2, GP, C0)
        ws_staged = staged(3, P, 2)

        spread_flat = x0_spread[:, :, :].rearrange("p c n -> p (c n)")
        h1 = spread_flat[:, 0:M1 * BATCH].rearrange("p (m n) -> p m n", m=M1)
        h2 = spread_flat[:, M1 * BATCH:(M1 + M2) * BATCH].rearrange("p (m n) -> p m n", m=M2)
        y = spread_flat[0:1, (M1 + M2) * BATCH:(M1 + M2 + 1) * BATCH]

        ps = ctx.enter_context(nc.psum_tensor("ps", [P, 8, BANK], F32))
        ps0, ps1, ps2 = (ps[:, i, :] for i in range(3))
        rep_ps = ps[0:GP, 3, :]
        x1 = ps[:, 4, :]
        x2 = ps[:, 5, :]

        ids_loaded = sem("ids_loaded")
        rows_ready = sem("rows_ready")
        rows_seen = sem("rows_seen")
        tile_gathered = sem("tile_gathered")
        leaving_ready = sem("leaving_ready")
        x0_written = sem("x0_written")
        rep_loaded = sem("rep_loaded")
        rep_ready = sem("rep_ready")
        rot_loaded = sem("rot_loaded")
        spread_loaded = {letter: sem("spread_loaded_" + letter) for letter in SPREAD}
        w0_loaded = sem("w0_loaded")
        w0b_loaded = sem("w0b_loaded")
        w0b_zeroed = sem("w0b_zeroed")
        w0_ready = sem("w0_ready")
        w1_loaded = sem("w1_loaded")
        w2_loaded = sem("w2_loaded")
        ws_loaded = sem("ws_loaded")
        whi_ready = sem("whi_ready")
        wlo_ready = sem("wlo_ready")
        biases_loaded = sem("biases_loaded")
        top_loaded = sem("top_loaded")
        prod_ready = sem("prod_ready")
        hi_ready = sem("hi_ready")
        own_lo_ready = sem("own_lo_ready")
        pool_lo_ready = sem("pool_lo_ready")
        used = {NATIVE: sem("native_used"), OWN: sem("own_used"), POOL: sem("pool_used"),
                STACKED: sem("stacked_used")}
        x1_ready = sem("x1_ready")
        x2_ready = sem("x2_ready")
        direct0_ready = sem("direct0_ready")
        direct1_ready = sem("direct1_ready")
        direct2_ready = sem("direct2_ready")
        sum01_done = sem("sum01_done")
        sum2_done = sem("sum2_done")
        h1_done = sem("h1_done")
        h1_ready = sem("h1_ready")
        h2_done = sem("h2_done")
        h2_ready = sem("h2_ready")
        y_done = sem("y_done")
        y_ready = sem("y_ready")
        out_written = sem("out_written")

        def x0_rows(t, first, pattern):
            return bass.AP(tensor=x0_dram.tensor, offset=t * (2 * FIELDS * TILE) + first, ap=pattern)

        block = ctx.enter_context(nc.Block())

        @block.gpsimd
        def _(pool):
            def low_parts(t, unit):
                _, first, end = UNITS[unit]
                i = POOL_LOWS[0 if t is START else 1].index(unit) % POOL_RING
                pool.wait_ge(hi_ready, count(HIGHS, t, unit))
                nc.gpsimd.tensor_tensor(pool_lo[:, i, 0:end - first, :], prod[:, slot(t, unit), 0:end - first, :],
                                        pool_hi[:, i, 0:end - first, :].bitcast(F32), ALU.subtract
                                        ).then_inc(pool_lo_ready, 1)

            def look_up(t):
                nc.gpsimd.tensor_tensor(rows_sb[:], ids_sb[:, bass.ds(t * SLOTS, SLOTS)], offsets_sb[:],
                                        ALU.add).then_inc(rows_ready, 1)
                pool.wait_ge(rows_ready, t + 1)
                pool.sem_inc(rows_seen, 1)

            def gather(first, end):
                for j in range(first, end):
                    nc.gpsimd.indirect_dma_start(
                        gathered[:, DIM * j:DIM * (j + 1)], None, table[:, :],
                        bass.IndirectOffsetOnAxis(ap=rows_sb[:, j:j + 1], axis=0),
                    ).then_inc(tile_gathered, 16)

            pool.wait_ge(ids_loaded, 32)
            look_up(0)
            gather(0, SLOTS)
            pool.wait_ge(leaving_ready, 1)
            look_up(1)
            gather(0, SLOTS)
            low_parts(START, "1b")
            pool.wait_ge(leaving_ready, 2)
            look_up(2)
            gather(0, 2)
            low_parts(START, "1d")
            gather(2, SLOTS)
            with pool.Fori(0, TILES - 3) as t:
                low_parts(t, "2b")
                pool.wait_ge(leaving_ready, t + 3)
                look_up(t + 3)
                gather(0, 1)
                low_parts(t, "2d")
                low_parts(t, "1b")
                gather(1, 3)
                low_parts(t, "1d")
                gather(3, SLOTS)
            with pool.Fori(TILES - 3, TILES - 1) as t:
                for unit in POOL_LOWS[1]:
                    low_parts(t, unit)
            for unit in POOL_LOWS[2]:
                low_parts(END, unit)

        @block.sync
        def _(sp):
            def group(g):
                return slice(FIELDS * g, FIELDS * (g + 1)), -(-(ROTATIONS - g) // GROUPS)

            sp.dma_start(ids_sb[:], ids).then_inc(ids_loaded, 16)
            sp.dma_start(offsets_sb[:], offsets).then_inc(ids_loaded, 16)
            for g in range(GROUPS):
                rows, n = group(g)
                sp.dma_start(w0_sb[rows, 0:n, :], w0a[g::GROUPS].rearrange("c i s -> i c s")).then_inc(w0_loaded, 16)
            sp.wait_ge(w0b_zeroed, 1)
            for g in range(GROUPS):
                rows, n = group(g)
                first = 1 if g == 0 else 0
                sp.dma_start(w0b_staged[rows, first:n, :],
                             w0b[g + GROUPS * first::GROUPS].rearrange("c i s -> i c s")).then_inc(w0b_loaded, 16)
            for i, w, w_staged, w_sb, loaded in ((1, w1, w1_staged, w1_sb, w1_loaded),
                                                 (2, w2, w2_staged, w2_sb, w2_loaded)):
                whole = w[0:(C1 - 1) * P, :].rearrange("(c p) s -> p c s", p=P)
                sp.dma_start(w_staged, whole[:, 0:SPLIT[i], :]).then_inc(loaded, 16)
                sp.dma_start(w_sb[:, :, :], whole[:, SPLIT[i]:, :]).then_inc(loaded, 16)
                for g in range(2):
                    sp.dma_start(ws_staged[HALF * g:HALF * (g + 1), i - 1, :], w[(C1 - 1) * P:, :]).then_inc(ws_loaded, 16)
            for b, b_sb in ((b0, b0_sb), (b1, b1_sb), (b2, b2_sb)):
                sp.dma_start(b_sb[:], b.rearrange("(s a) -> s a", a=1)).then_inc(biases_loaded, 16)

            def write_x0(tile):
                sp.wait_ge(leaving_ready, tile + 1)
                for r in reversed(range(GROUPS)):
                    n = DIM * (SLOTS if r < GROUPS - 1 else LAST_SLOTS)
                    sp.dma_start(x0_rows(tile, r * SLOTS * DIM, [[TILE, FIELDS], [FIELDS * TILE, 2], [1, n]]),
                                 leaving[FIELDS * r:FIELDS * (r + 1), 0:n].unsqueeze(1).to_broadcast([FIELDS, 2, n])
                                 ).then_inc(x0_written, 16)

            def load_rotations(t):
                for g in range(GROUPS):
                    rows, _ = group(g)
                    sp.dma_start(x0_rep[rows, :], x0_rows(t, 0, [[TILE, FIELDS], [1, TILE]])).then_inc(rep_loaded, 16)
                for g in range(GROUPS):
                    rows, n = group(g)
                    sp.dma_start(x0_rot[rows, 0:n, :],
                                 x0_rows(t, g * TILE, [[TILE, FIELDS], [GROUPS * TILE, n], [1, TILE]])
                                 ).then_inc(rot_loaded, 16)

            def load_spread(t, letter):
                c, end = SPREAD[letter]
                for g in (1, 0):
                    n = min(end, (FIELDS - g + 1) // 2) - c
                    sp.dma_start(x0_spread[HALF * g:HALF * (g + 1), c:c + n, :],
                                 x0_rows(t, (2 * c + g) * TILE, [[0, HALF], [2 * TILE, n], [1, TILE]])
                                 ).then_inc(spread_loaded[letter], 16)
                if end == C1:
                    sp.dma_start(x0_spread[HALF:P, end - 1, :], x0_rows(t, (FIELDS - 1) * TILE, [[0, HALF], [1, TILE]])
                                 ).then_inc(spread_loaded[letter], 16)

            def reload_spread(t, letter):
                sp.wait_ge(prod_ready, count(FORMED, t, "2" + letter))
                load_spread(t + 1, letter)

            def reload_rotations(t, turn, ahead):
                sp.wait_ge(prod_ready, count(FORMED, turn, "0b"))
                sp.wait_ge(x0_written, 16 * GROUPS * t + 16 * GROUPS * (ahead + 1))
                load_rotations(t + ahead)

            write_x0(0)
            sp.wait_ge(x0_written, 16 * GROUPS)
            load_rotations(0)
            for letter in SPREAD:
                load_spread(0, letter)
            write_x0(1)
            for dst, src in ((ctx_sb[:], ctx_t),
                             (wt1_sb[:], wt1[0:2 * P, :].rearrange("(c p) n -> p c n", p=P)),
                             (wt1c_sb[:], wt1[2 * P:, :]),
                             (wt2_sb[:], wt2.rearrange("(c p) n -> p c n", p=P)),
                             (wt3_sb[:], wt3), (bt1_sb[:], bt1), (bt2_sb[:], bt2)):
                sp.dma_start(dst, src).then_inc(top_loaded, 16)
            reload_rotations(0, START, 1)

            def reload(t):
                for letter in "abcd":
                    reload_spread(t, letter)
                write_x0(t + 2)
                reload_spread(t, "e")
                reload_rotations(t, t, 2)

            with sp.Fori(0, TILES - 2) as t:
                reload(t)
            for letter in SPREAD:
                reload_spread(TILES - 2, letter)

            sp.wait_ge(y_ready, NH)
            sp.dma_start(out.rearrange("b a -> a b"), y).then_inc(out_written, 16)
            sp.wait_ge(out_written, 16)

        @block.vector
        def _(dve):
            dve.sem_inc(sum01_done, 1)
            dve.sem_inc(sum2_done, 1)
            nc.vector.memset(w0b_staged[:, 0, :], 0.0).then_inc(w0b_zeroed, 1)
            dve.wait_ge(w0_loaded, 16 * GROUPS)
            dve.wait_ge(w0b_loaded, 16 * GROUPS)
            nc.vector.tensor_tensor(w0_sb[:, 0:C0 - 1, :], w0_sb[:, 0:C0 - 1, :], w0b_staged[:, 0:C0 - 1, :],
                                    ALU.add).then_inc(w0_ready, 1)
            rows = C0_ROWS[C0 - 1]
            nc.vector.tensor_tensor(w0_sb[0:rows, C0 - 1, :], w0_sb[0:rows, C0 - 1, :], w0b_staged[0:rows, C0 - 1, :],
                                    ALU.add).then_inc(w0_ready, 1)
            for i, (w, w_hi, w_lo) in enumerate(((w0_sb[:, 0:SPLIT[0], :], w0_hi, w0_lo),
                                                 (w1_staged, w1_hi, w1_lo), (w2_staged, w2_hi, w2_lo),
                                                 (ws_staged[0:HALF], ws_hi[0:HALF], ws_lo))):
                dve.wait_ge(whi_ready, i + 1)
                nc.vector.tensor_tensor(w_lo[:], w, w_hi[:].bitcast(F32), ALU.subtract).then_inc(wlo_ready, 1)

            dve.wait_ge(wlo_ready, 4)

            def products(t, unit, chunk_rows, left, right):
                units = FORMED[0] if t is START else FORMED[1] + FORMED[2 if t is END else 1]
                place = len(units) - 1 - units[::-1].index(unit) - RING
                if place >= 0:
                    holder = units[place]
                    ago = int(t is not START and place < len(FORMED[1]))
                    if UNITS[holder][0] == NATIVE:
                        dve.wait_ge(used[NATIVE], count(TAKEN, t, holder, [NATIVE], ago))
                    elif UNITS[holder][0] == OWN:
                        dve.wait_ge(own_lo_ready, count(OWN_LOWS, t, holder, ago=ago))
                    else:
                        dve.wait_ge(pool_lo_ready, count(POOL_LOWS, t, holder, ago=ago))
                    if holder[1] == "e":
                        dve.wait_ge(own_lo_ready, count(OWN_LOWS, t, holder[0] + "s", ago=ago))
                _, first, end = UNITS[unit]
                end += unit[1] == "e"
                full = sum(chunk_rows[c] == chunk_rows[0] for c in range(first, end))
                for c, m in ((first, full), (first + full, end - first - full)):
                    if m:
                        rows = chunk_rows[c]
                        last = nc.vector.tensor_tensor(prod[0:rows, slot(t, unit), c - first:c - first + m, :],
                                                       left(rows, c, m), right(rows, c, m), ALU.mult)
                last.then_inc(prod_ready, 1)

            def low_parts(t, unit, rows=P):
                _, first, end = UNITS[unit]
                dve.wait_ge(hi_ready, count(HIGHS, t, unit))
                nc.vector.tensor_tensor(own_lo[0:rows, 0:end - first, :], prod[0:rows, slot(t, unit), 0:end - first, :],
                                        own_hi[0:rows, 0:end - first, :].bitcast(F32), ALU.subtract
                                        ).then_inc(own_lo_ready, 1)

            def stacked_low_parts(t, unit):
                dve.wait_ge(hi_ready, count(HIGHS, t, unit))
                nc.vector.tensor_tensor(stacked[HALF:P, :], prod[HALF:P, slot(t, unit[0] + "e"), UNIT - 1, :],
                                        stacked[HALF:P, :].bitcast(F32), ALU.subtract).then_inc(own_lo_ready, 1)

            def same(x):
                return lambda rows, c, m: x[0:rows, :].unsqueeze(1).to_broadcast([rows, m, TILE])

            def chunks_of(x):
                return lambda rows, c, m: x[0:rows, c:c + m, :]

            def layer0(t, tile):
                dve.wait_ge(rep_ready, tile + 1)
                dve.wait_ge(rot_loaded, 16 * GROUPS * (tile + 1))
                for unit in ("0a", "0b"):
                    products(t, unit, C0_ROWS, chunks_of(x0_rot), same(rep_ps))
                low_parts(t, "0a", GP)

            def form(t, tile, unit, x):
                if x is x1:
                    letter = unit[1]
                    dve.wait_ge(spread_loaded[letter], (48 if letter == "e" else 32) * (tile + 1))
                products(t, unit, C1_ROWS, chunks_of(x0_spread), same(x))

            def sum_dims(z_out, src):
                return nc.vector.tensor_reduce(z_out, src.rearrange("p (b d) -> p b d", d=DIM), AX_X, ALU.add)

            def sum01(t):
                dve.wait_ge(direct0_ready, t + 1)
                dve.wait_ge(direct1_ready, t + 1)
                sum_dims(z[:, 0, bass.ds(t * SAMPLES, SAMPLES)], direct01[:, :]).then_inc(sum01_done, 1)

            def sum2(t):
                dve.wait_ge(direct2_ready, t + 2)
                sum_dims(z[:, 1, bass.ds(t * SAMPLES, SAMPLES)], direct2[:, :]).then_inc(sum2_done, 1)

            layer0(START, 0)
            dve.wait_ge(x1_ready, 2)
            for unit in ("1a", "1b", "1c", "1d"):
                form(START, 0, unit, x1)
            low_parts(START, "1c")
            form(START, 0, "1e", x1)
            stacked_low_parts(START, "1s")
            dve.wait_ge(pool_lo_ready, 1)
            with dve.Fori(0, TILES - 1) as t:
                layer0(t, t + 1)
                dve.wait_ge(x2_ready, 2 * (t + 1))
                for unit in ("2a", "2b", "2c", "2d"):
                    form(t, t, unit, x2)
                sum01(t)
                dve.wait_ge(x1_ready, 2 * (t + 2))
                form(t, t + 1, "1a", x1)
                form(t, t + 1, "1b", x1)
                form(t, t, "2e", x2)
                form(t, t + 1, "1c", x1)
                stacked_low_parts(t, "2s")
                form(t, t + 1, "1d", x1)
                low_parts(t, "1c")
                form(t, t + 1, "1e", x1)
                sum2(t)
                stacked_low_parts(t, "1s")
            last = TILES - 1
            dve.wait_ge(x2_ready, 2 * TILES)
            for unit in ("2a", "2b", "2c", "2d", "2e"):
                form(END, last, unit, x2)
            stacked_low_parts(END, "2s")
            sum01(last)
            sum2(last)
            for n in range(NH):
                dve.wait_ge(y_done, n + 1)
                nc.vector.tensor_copy(y[:, BANK * n:BANK * (n + 1)], ps[0:1, n, :]).then_inc(y_ready, 1)

        @block.tensor
        def _(pe):
            LAYERS = ((C0_ROWS, w0_sb, 0, w0_hi, w0_lo, ps0),
                      (C1_ROWS, w1_sb, SPLIT[1], w1_hi, w1_lo, ps1),
                      (C1_ROWS, w2_sb, SPLIT[2], w2_hi, w2_lo, ps2))

            def contract(t, unit):
                layer = int(unit[0])
                chunk_rows, w_native, native_first, w_hi, w_lo, out_ps = LAYERS[layer]
                of_layer = [u for u in TAKEN[0 if t is START else 2 if t is END else 1] if u[0] == unit[0]]
                start, stop = unit == of_layer[0], unit == of_layer[-1]
                kind, first, end = UNITS[unit]
                if kind == NATIVE:
                    pe.wait_ge(prod_ready, count(FORMED, t, unit))
                elif kind == POOL:
                    pe.wait_ge(pool_lo_ready, count(POOL_LOWS, t, unit))
                else:
                    pe.wait_ge(own_lo_ready, count(OWN_LOWS, t, unit))
                if kind == STACKED:
                    nc.tensor.matmul(out_ps, ws_hi[:, layer - 1, :], stacked[:, :], start=start, stop=False)
                    mm = nc.tensor.matmul(out_ps, ws_lo[:, layer - 1, :], stacked[0:HALF, :], start=False, stop=stop)
                    mm.then_inc(used[STACKED], 1)
                    return
                i = (count(POOL_LOWS, t if t is START or t is END else 0, unit) - 1) % POOL_RING if kind == POOL else 0
                for c in range(first, end):
                    rows = slice(0, chunk_rows[c])
                    begin, finish = start and c == first, stop and c == end - 1
                    if kind == NATIVE:
                        mm = nc.tensor.matmul(out_ps, w_native[rows, c - native_first, :],
                                              prod[rows, slot(t, unit), c - first, :], start=begin, stop=finish)
                    else:
                        hi, lo = ((own_hi[rows, c - first, :], own_lo[rows, c - first, :]) if kind == OWN else
                                  (pool_hi[rows, i, c - first, :], pool_lo[rows, i, c - first, :]))
                        nc.tensor.matmul(out_ps, w_hi[rows, c, :], lo, start=begin, stop=False)
                        nc.tensor.matmul(out_ps, w_lo[rows, c, :], hi, start=False, stop=False)
                        mm = nc.tensor.matmul(out_ps, w_hi[rows, c, :], hi, start=False, stop=finish)
                mm.then_inc(used[kind], 1)

            pe.wait_ge(w0_ready, 2)
            pe.wait_ge(wlo_ready, 4)
            pe.wait_ge(w1_loaded, 32)
            pe.wait_ge(w2_loaded, 32)
            for unit in TAKEN[0]:
                contract(START, unit)
            with pe.Fori(0, TILES - 1) as t:
                for unit in TAKEN[1]:
                    if unit == "0b":
                        pe.wait_ge(direct0_ready, t + 1)
                    elif unit == "2a":
                        pe.wait_ge(direct2_ready, t + 1)
                    elif unit == "1a":
                        pe.wait_ge(direct1_ready, t + 1)
                    contract(t, unit)
            pe.wait_ge(direct2_ready, TILES)
            for unit in TAKEN[2]:
                contract(END, unit)

            pe.wait_ge(top_loaded, 16 * 7)
            pe.wait_ge(direct2_ready, TILES + 1)
            pe.wait_ge(sum01_done, TILES + 1)
            pe.wait_ge(sum2_done, TILES + 1)
            for n in range(NH):
                cols = slice(BANK * n, BANK * (n + 1))
                for m in range(M1):
                    outs = slice(P * m, P * (m + 1))
                    nc.tensor.matmul(ps[:, M1 * n + m, :], wt1_sb[:, 0, outs], z[:, 0, cols], start=True, stop=False)
                    nc.tensor.matmul(ps[:, M1 * n + m, :], wt1_sb[:, 1, outs], z[:, 1, cols], start=False, stop=False)
                    nc.tensor.matmul(ps[:, M1 * n + m, :], wt1c_sb[:, outs], ctx_sb[:, cols],
                                     start=False, stop=True).then_inc(h1_done, 1)
            for n in range(NH):
                for m in range(M2):
                    pe.wait_ge(h1_ready, M1 * (n + 1))
                    for c in range(M1):
                        mm = nc.tensor.matmul(ps[:, M1 * n + m, :], wt2_sb[:, c, P * m:P * (m + 1)],
                                              h1[:, c, BANK * n:BANK * (n + 1)], start=(c == 0), stop=(c == M1 - 1))
                    mm.then_inc(h2_done, 1)
            for n in range(NH):
                pe.wait_ge(h2_ready, M2 * (n + 1))
                for c in range(M2):
                    mm = nc.tensor.matmul(ps[0:1, n, :], wt3_sb[:, c:c + 1], h2[:, c, BANK * n:BANK * (n + 1)],
                                          start=(c == 0), stop=(c == M2 - 1))
                mm.then_inc(y_done, 1)

        @block.scalar
        def _(act):
            def relu(dst, src, bias):
                return nc.scalar.activation(dst, src, ACT.Relu, bias=bias)

            def copy(dst, src):
                return nc.scalar.activation(dst, src, ACT.Copy)

            LOW, HIGH = slice(0, HALF), slice(HALF, SIZE)

            def high_parts(t, unit, rows=P):
                kind, first, end = UNITS[unit]
                formed = unit[0] + "e" if kind == STACKED else unit
                act.wait_ge(prod_ready, count(FORMED, t, formed))
                ring = POOL_RING if kind == POOL else 1
                n = count(TAKEN, t if t is START or t is END else 0, unit, [kind])
                if n > ring:
                    act.wait_ge(used[kind], count(TAKEN, t, unit, [kind]) - ring)
                if kind == STACKED:
                    dst, src = stacked[:, :], prod[:, slot(t, formed), UNIT - 1, :]
                else:
                    hi = own_hi if kind == OWN else pool_hi[:, (n - 1) % POOL_RING, :, :]
                    dst, src = hi[0:rows, 0:end - first, :], prod[0:rows, slot(t, unit), 0:end - first, :]
                copy(dst, src).then_inc(hi_ready, 1)

            def take_x0(tile, first=False):
                act.wait_ge(tile_gathered, 16 * SLOTS * (tile + 1))
                if not first:
                    act.wait_ge(x0_written, 16 * GROUPS * tile)
                copy(leaving[:], gathered[:]).then_inc(leaving_ready, 1)

            def copy_rep(tile):
                act.wait_ge(rep_loaded, 16 * GROUPS * (tile + 1))
                copy(rep_ps, x0_rep[:, :]).then_inc(rep_ready, 1)

            def next_factor(out_ps, bias, x, x_ready):
                for half in (LOW, HIGH):
                    relu(x[half, :], out_ps[LOW, :], bias[LOW, :]).then_inc(x_ready, 1)

            def direct_outputs(tile, out_ps, bias, direct, direct_ready):
                act.wait_ge(sum01_done, tile + 1)
                relu(direct, out_ps[HIGH, :], bias[HIGH, :]).then_inc(direct_ready, 1)

            def factor1(t):
                act.wait_ge(used[OWN], count(TAKEN, t, "0a", [OWN]))
                next_factor(ps0, b0_sb, x1, x1_ready)

            def direct0(tile):
                direct_outputs(tile, ps0, b0_sb, direct01[LOW, :], direct0_ready)

            def outputs1(t, tile):
                act.wait_ge(used[STACKED], count(TAKEN, t, None, [STACKED]))
                next_factor(ps1, b1_sb, x2, x2_ready)
                direct_outputs(tile, ps1, b1_sb, direct01[HIGH, :], direct1_ready)

            def outputs2(t, tile):
                act.wait_ge(used[STACKED], count(TAKEN, t, "2s", [STACKED]))
                act.wait_ge(sum2_done, tile + 1)
                relu(direct2[:, :], ps2, b2_sb[:, :]).then_inc(direct2_ready, 1)

            act.sem_inc(direct2_ready, 1)
            act.wait_ge(w0_ready, 1)
            copy(w0_hi[:], w0_sb[:, 0:SPLIT[0], :]).then_inc(whi_ready, 1)
            act.wait_ge(w1_loaded, 32)
            copy(w1_hi[:], w1_staged).then_inc(whi_ready, 1)
            act.wait_ge(w2_loaded, 32)
            copy(w2_hi[:], w2_staged).then_inc(whi_ready, 1)
            act.wait_ge(ws_loaded, 64)
            copy(ws_hi[:], ws_staged).then_inc(whi_ready, 1)
            act.wait_ge(biases_loaded, 16 * 3)

            take_x0(0, first=True)
            copy_rep(0)
            high_parts(START, "0a", GP)
            take_x0(1)
            factor1(START)
            direct0(0)
            for unit in ("1b", "1c", "1d", "1s"):
                high_parts(START, unit)
            def turn(t, writes):
                copy_rep(t + 1)
                high_parts(t, "0a", GP)
                outputs1(t, t)
                high_parts(t, "2b")
                if writes:
                    take_x0(t + 2)
                factor1(t)
                direct0(t + 1)
                high_parts(t, "2d")
                high_parts(t, "1b")
                high_parts(t, "2s")
                high_parts(t, "1c")
                high_parts(t, "1d")
                outputs2(t, t)
                high_parts(t, "1s")

            with act.Fori(0, TILES - 2) as t:
                turn(t, True)
            turn(TILES - 2, False)
            outputs1(END, TILES - 1)
            for unit in ("2b", "2d", "2s"):
                high_parts(END, unit)
            outputs2(END, TILES - 1)

            act.wait_ge(top_loaded, 16 * 7)
            for n in range(NH):
                for m in range(M1):
                    act.wait_ge(h1_done, M1 * n + m + 1)
                    relu(h1[:, m, BANK * n:BANK * (n + 1)], ps[:, M1 * n + m, :], bt1_sb[:, m:m + 1]).then_inc(h1_ready, 1)
            for n in range(NH):
                for m in range(M2):
                    act.wait_ge(h2_done, M2 * n + m + 1)
                    relu(h2[:, m, BANK * n:BANK * (n + 1)], ps[:, M1 * n + m, :], bt2_sb[:, m:m + 1]).then_inc(h2_ready, 1)


def kernel(**inputs):
    import numpy as np
    import concourse.bacc as bacc
    from concourse.bass_utils import run_bass_kernel_spmd

    a = {k: np.asarray(v) for k, v in inputs.items()}
    tables = [a[f"tbl_{f}"] for f in range(FIELDS)]
    starts = np.cumsum([0] + [t.shape[0] for t in tables[:-1]]).astype(np.int32)

    sample = np.minimum(np.arange(GROUPS)[:, None] * SLOTS + np.arange(SLOTS)[None, :], SAMPLES - 1)
    ids = a["ids"].reshape(TILES, SAMPLES, FIELDS)[:, sample, :]
    ids = ids.transpose(1, 3, 0, 2).reshape(GP, TILES * SLOTS)
    offsets = np.broadcast_to(np.tile(starts, GROUPS)[:, None], (GP, SLOTS))

    i = np.arange(FIELDS)[None, :]
    k = (i + np.arange(ROTATIONS)[:, None]) % FIELDS
    w0 = a["L0_rec_w0"]
    host = {
        "table": np.concatenate(tables, axis=0),
        "ids": ids, "offsets": offsets,
        "ctx_t": a["dense_ctx"].T,
        "w0a": w0[i, k], "w0b": w0[k, i],
        "w1": a["L0_rec_w1"].reshape(FIELDS * HALF, SIZE),
        "w2": a["L0_rec_w2"].reshape(FIELDS * HALF, SIZE),
        "b0": a["L0_rec_b0"], "b1": a["L0_rec_b1"], "b2": a["L0_rec_b2"],
        "wt1": a["W_top1"], "bt1": a["b_top1"].reshape(M1, P).T,
        "wt2": a["W_top2"], "bt2": a["b_top2"].reshape(M2, P).T,
        "wt3": a["W_top3"].reshape(M2, P).T,
    }
    host = {k_: np.ascontiguousarray(v) for k_, v in host.items()}
    nc = bacc.Bacc("TRN2", target_bir_lowering=False, num_devices=1)
    args = [nc.dram_tensor(k_, v.shape, mybir.dt.from_np(v.dtype), kind="ExternalInput").ap() for k_, v in host.items()]
    args.append(nc.dram_tensor("out", (BATCH, 1), F32, kind="ExternalOutput").ap())
    tower(nc, *args)
    result = run_bass_kernel_spmd(nc, [host], core_ids=[0])
    return result.results[0]["out"]
```

```python
from contextlib import ExitStack

import concourse.bass as bass
from concourse import mybir

F32 = mybir.dt.float32
F32R = mybir.dt.float32r
I32 = mybir.dt.int32
ALU = mybir.AluOpType
ACT = mybir.ActivationFunctionType
AX_X = mybir.AxisListType.X

P = 128
FIELDS = 39
DIM = 16
BATCH = 1024
SIZE = 128
HALF = SIZE // 2
TILE = 512
SAMPLES = TILE // DIM
TILES = BATCH // SAMPLES

GROUPS = P // FIELDS
GP = GROUPS * FIELDS
SLOTS = -(-SAMPLES // GROUPS)
LAST_SLOTS = SAMPLES - (GROUPS - 1) * SLOTS

ROTATIONS = FIELDS // 2 + 1
C0 = -(-ROTATIONS // GROUPS)
C0_ROWS = [FIELDS * len(range(c, ROTATIONS, C0)) for c in range(C0)]
C1 = -(-FIELDS // 2)
C1_ROWS = [P] * C1
UNIT = 4

NATIVE, OWN, POOL, STACKED = range(4)
UNITS = {
    "0a": (OWN, 0, 3), "0b": (NATIVE, 3, C0),
    "1a": (NATIVE, 12, 16), "1b": (POOL, 0, 4), "1c": (OWN, 8, 12), "1d": (POOL, 4, 8),
    "1e": (NATIVE, 16, C1 - 1), "1s": (STACKED, C1 - 1, C1),
    "2a": (NATIVE, 12, 16), "2b": (POOL, 0, 4), "2c": (NATIVE, 8, 12), "2d": (POOL, 4, 8),
    "2e": (NATIVE, 16, C1 - 1), "2s": (STACKED, C1 - 1, C1),
}
SPLIT = [3, 12, 8]
SPREAD = {u[1]: UNITS[u][1:] for u in ("1a", "1b", "1c", "1d")}
SPREAD["e"] = (16, C1)

START, END = "start", "end"
FORMED = (["0a", "0b", "1a", "1b", "1c", "1d", "1e"],
          ["0a", "0b", "2b", "2a", "2c", "2d", "1a", "1b", "2e", "1c", "1d", "1e"],
          ["2b", "2a", "2d", "2c", "2e"])
HIGHS = (["0a", "1b", "1c", "1d", "1s"],
         ["0a", "2b", "2d", "1b", "2s", "1c", "1d", "1s"],
         ["2b", "2d", "2s"])
OWN_LOWS = (["0a", "1c", "1s"],
            ["0a", "2s", "1c", "1s"],
            ["2s"])
POOL_LOWS = (["1b", "1d"],
             ["2b", "2d", "1b", "1d"],
             ["2b", "2d"])
TAKEN = (["0b", "0a", "1a", "1b", "1c", "1e", "1d", "1s"],
         ["0b", "0a", "2a", "2c", "2b", "1a", "2d", "2e", "2s", "1b", "1c", "1e", "1d", "1s"],
         ["2a", "2c", "2b", "2d", "2e", "2s"])
RING = 4
POOL_RING = 2


def count(steps, t, unit=None, kinds=range(4), ago=0):
    start, turn, end = steps

    def of_kinds(units):
        return sum(UNITS[u][0] in kinds for u in units)

    def upto(units):
        return of_kinds(units[:units.index(unit) + 1]) if unit else 0

    if t is START:
        return upto(start)
    if t is END:
        return of_kinds(start) + of_kinds(turn) * (TILES - 1 - ago) + upto(turn if ago else end)
    return of_kinds(start) + upto(turn) - of_kinds(turn) * ago + t * of_kinds(turn)


def slot(t, unit):
    return (count(FORMED, t if t is START or t is END else 0, unit) - 1) % RING


assert len(FORMED[1]) % RING == 0
assert [UNITS[u][0] for u in FORMED[0][1 - RING:]] == [UNITS[u][0] for u in FORMED[1][1 - RING:]]

H1 = 512
H2 = 256
CTX = 16
TOP_LOADS = 11
M1 = H1 // P
M2 = H2 // P
BANK = 512
NH = BATCH // BANK
Z_COLS = (slice(0, BANK), slice(BANK, BATCH - SAMPLES), slice(BATCH - SAMPLES, BATCH))


def tower(nc, table, ids, offsets, ctx_t, w0a, w0b, w1, w2, b0, b1, b2, wt1, bt1, wt2, bt2, wt3, out):
    with ExitStack() as ctx:
        def sb(name, shape, dt=F32):
            return ctx.enter_context(nc.sbuf_tensor(name, shape, dt))

        def sem(name):
            return ctx.enter_context(nc.semaphore(name))

        x0_dram = nc.dram_tensor("x0_rows", [1 + TILES * 2 * FIELDS, TILE], F32, kind="Internal").ap()

        ids_sb = sb("ids_sb", [GP, TILES * SLOTS], I32)
        offsets_sb = sb("offsets_sb", [GP, SLOTS], I32)
        rows_sb = sb("rows_sb", [GP, SLOTS], I32)
        gathered = sb("gathered", [GP, SLOTS * DIM])
        leaving = sb("leaving", [GP, SLOTS * DIM])
        x0_rep = sb("x0_rep", [GP, TILE])
        prod = sb("prod", [P, RING, UNIT, TILE])
        own_hi = sb("own_hi", [P, UNIT, TILE], F32R)
        own_lo = sb("own_lo", [P, UNIT, TILE], F32R)
        pool_hi = sb("pool_hi", [P, POOL_RING, UNIT, TILE], F32R)
        pool_lo = sb("pool_lo", [P, POOL_RING, UNIT, TILE], F32R)
        stacked = sb("stacked", [P, TILE], F32R)
        direct01 = sb("direct01", [P, TILE])
        direct2 = sb("direct2", [P, TILE])
        w0_sb = sb("w0_sb", [GP, C0, SIZE])
        w1_sb = sb("w1_sb", [P, C1 - 1 - SPLIT[1], SIZE])
        w2_sb = sb("w2_sb", [P, C1 - 1 - SPLIT[2], SIZE])
        w0_hi = sb("w0_hi", [GP, SPLIT[0], SIZE], F32R)
        w0_lo = sb("w0_lo", [GP, SPLIT[0], SIZE], F32R)
        w1_hi = sb("w1_hi", [P, SPLIT[1], SIZE], F32R)
        w1_lo = sb("w1_lo", [P, SPLIT[1], SIZE], F32R)
        w2_hi = sb("w2_hi", [P, SPLIT[2], SIZE], F32R)
        w2_lo = sb("w2_lo", [P, SPLIT[2], SIZE], F32R)
        ws_hi = sb("ws_hi", [P, 2, SIZE], F32R)
        ws_lo = sb("ws_lo", [HALF, 2, SIZE], F32R)
        b0_sb = sb("b0_sb", [P, 1])
        b1_sb = sb("b1_sb", [P, 1])
        b2_sb = sb("b2_sb", [P, 1])
        z = sb("z", [P, 2, BATCH])
        ctx_sb = sb("ctx_sb", [3 * CTX, BATCH])
        wt1_sb = sb("wt1_sb", [P, 2, H1])
        wt1c_sb = sb("wt1c_sb", [3 * CTX, H1])
        wt2_sb = sb("wt2_sb", [P, M1, H2])
        wt3_sb = sb("wt3_sb", [P, M2])
        bt1_sb = sb("bt1_sb", [P, M1])
        bt2_sb = sb("bt2_sb", [P, M2])

        def staged(slot, rows, chunks):
            return prod[0:rows, slot, :, :].rearrange("p u n -> p (u n)")[:, 0:chunks * SIZE].rearrange(
                "p (c s) -> p c s", s=SIZE)

        w1_staged, w2_staged, w0b_staged = staged(0, P, SPLIT[1]), staged(1, P, SPLIT[2]), staged(2, GP, C0)
        ws_staged = staged(3, P, 2)

        with ExitStack() as passing:
            x0_rot = passing.enter_context(
                nc.sbuf_tensor("x0_rot", [GP, C0, TILE], F32))
            x0_spread = passing.enter_context(
                nc.sbuf_tensor("x0_spread", [P, C1, TILE], F32))
        z_hi = sb("z_hi", [P, 2, BATCH], F32R)
        ctx_parts = sb("ctx_parts", [3 * CTX, BATCH], F32R)
        wt1c_parts = sb("wt1c_parts", [3 * CTX, H1], F32R)
        h1_hi0 = sb("h1_hi0", [P, M1, BANK], F32R)
        h1_hi1 = sb("h1_hi1", [P, M1, BANK], F32R)
        h1_lo0 = sb("h1_lo0", [P, M1, BANK], F32R)
        h1 = sb("h1", [P, M1, BANK])
        h1_lo1 = sb("h1_lo1", [P, M1, BANK], F32R)
        h1_hi, h1_lo = (h1_hi0, h1_hi1), (h1_lo0, h1_lo1)
        own_hi_flat = own_hi[:, :, :].rearrange("p u n -> p (u n)")
        wt1_hi = own_hi_flat[:, 0:2 * H1].rearrange("p (c n) -> p c n", c=2)
        wt1_lo = own_hi_flat[:, 2 * H1:4 * H1].rearrange("p (c n) -> p c n", c=2)
        z_lo = own_lo[:, :, :].rearrange("p u n -> p (u n)").rearrange("p (c n) -> p c n", c=2)
        wt2_hi, wt2_lo = (x[:, 0, :, :].rearrange("p u n -> p (u n)")[:, 0:M1 * H2].rearrange(
            "p (c n) -> p c n", c=M1) for x in (pool_hi, pool_lo))
        wt1c_hi = x0_rep[0:3 * CTX, :].bitcast(F32R)
        h2 = prod[:, 1, :, :].rearrange("p (m h) n -> p m h n", h=NH)
        y = prod[0:1, 0, 0:NH, :]

        ps = ctx.enter_context(nc.psum_tensor("ps", [P, 8, BANK], F32))
        ps0, ps1, ps2 = (ps[:, i, :] for i in range(3))
        rep_ps = ps[0:GP, 3, :]
        x1 = ps[:, 4, :]
        x2 = ps[:, 5, :]
        BANKS1 = ((6, 7, 3, 4), (0, 1, 5, 2))
        BANKS2 = ((6, 7), (3, 4))
        BANKS3 = (6, 3)

        ids_loaded = sem("ids_loaded")
        rows_ready = sem("rows_ready")
        rows_seen = sem("rows_seen")
        tile_gathered = sem("tile_gathered")
        leaving_ready = sem("leaving_ready")
        x0_written = sem("x0_written")
        rep_loaded = sem("rep_loaded")
        rep_ready = sem("rep_ready")
        rot_loaded = {unit: sem("rot_loaded_" + unit) for unit in ("0a", "0b")}
        spread_loaded = {letter: sem("spread_loaded_" + letter) for letter in SPREAD}
        w0_loaded = sem("w0_loaded")
        w0b_loaded = sem("w0b_loaded")
        w0b_zeroed = sem("w0b_zeroed")
        w0_ready = sem("w0_ready")
        w1_loaded = sem("w1_loaded")
        w2_loaded = sem("w2_loaded")
        ws_loaded = sem("ws_loaded")
        whi_ready = sem("whi_ready")
        wlo_ready = sem("wlo_ready")
        biases_loaded = sem("biases_loaded")
        top_loaded = sem("top_loaded")
        prod_ready = sem("prod_ready")
        half_ready = sem("half_ready")
        hi_ready = sem("hi_ready")
        own_lo_ready = sem("own_lo_ready")
        pool_lo_ready = sem("pool_lo_ready")
        used = {NATIVE: sem("native_used"), OWN: sem("own_used"), POOL: sem("pool_used"),
                STACKED: sem("stacked_used")}
        x1_ready = sem("x1_ready")
        x2_ready = sem("x2_ready")
        direct0_ready = sem("direct0_ready")
        direct1_ready = sem("direct1_ready")
        direct2_ready = sem("direct2_ready")
        sum01_done = sem("sum01_done")
        sum2_done = sem("sum2_done")
        z_hi_ready = sem("z_hi_ready")
        z_lo_ready = sem("z_lo_ready")
        top_hi_ready = sem("top_hi_ready")
        top_lo_ready = sem("top_lo_ready")
        h1_done = sem("h1_done")
        h1_hi_ready = sem("h1_hi_ready")
        h1_lo_ready = sem("h1_lo_ready")
        h2_done = sem("h2_done")
        h2_ready = sem("h2_ready")
        y_done = sem("y_done")
        y_ready = sem("y_ready")
        out_written = sem("out_written")

        def x0_rows(t, first, pattern):
            return bass.AP(tensor=x0_dram.tensor, offset=t * (2 * FIELDS * TILE) + (TILE + first), ap=pattern)

        block = ctx.enter_context(nc.Block())

        @block.gpsimd
        def _(pool):
            def low_parts(t, unit):
                _, first, end = UNITS[unit]
                i = POOL_LOWS[0 if t is START else 1].index(unit) % POOL_RING
                pool.wait_ge(hi_ready, count(HIGHS, t, unit))
                nc.gpsimd.tensor_tensor(pool_lo[:, i, 0:end - first, :], prod[:, slot(t, unit), 0:end - first, :],
                                        pool_hi[:, i, 0:end - first, :].bitcast(F32), ALU.subtract
                                        ).then_inc(pool_lo_ready, 1)

            def look_up(t):
                nc.gpsimd.tensor_tensor(rows_sb[:], ids_sb[:, bass.ds(t * SLOTS, SLOTS)], offsets_sb[:],
                                        ALU.add).then_inc(rows_ready, 1)
                pool.wait_ge(rows_ready, t + 1)
                pool.sem_inc(rows_seen, 1)

            def gather(first, end):
                for j in range(first, end):
                    nc.gpsimd.indirect_dma_start(
                        gathered[:, DIM * j:DIM * (j + 1)], None, table[:, :],
                        bass.IndirectOffsetOnAxis(ap=rows_sb[:, j:j + 1], axis=0),
                    ).then_inc(tile_gathered, 16)

            pool.wait_ge(ids_loaded, 32)
            look_up(0)
            gather(0, SLOTS)
            pool.wait_ge(leaving_ready, 1)
            look_up(1)
            gather(0, SLOTS)
            low_parts(START, "1b")
            pool.wait_ge(leaving_ready, 2)
            look_up(2)
            gather(0, 2)
            low_parts(START, "1d")
            gather(2, SLOTS)
            with pool.Fori(0, TILES - 3) as t:
                low_parts(t, "2b")
                pool.wait_ge(leaving_ready, t + 3)
                look_up(t + 3)
                gather(0, 1)
                low_parts(t, "2d")
                low_parts(t, "1b")
                gather(1, 3)
                low_parts(t, "1d")
                gather(3, SLOTS)
            with pool.Fori(TILES - 3, TILES - 1) as t:
                for unit in POOL_LOWS[1]:
                    low_parts(t, unit)
            for unit in POOL_LOWS[2]:
                low_parts(END, unit)

        @block.sync
        def _(sp):
            def group(g):
                return slice(FIELDS * g, FIELDS * (g + 1)), C0 * g, min(C0 * (g + 1), ROTATIONS)

            sp.dma_start(ids_sb[:], ids).then_inc(ids_loaded, 16)
            sp.dma_start(offsets_sb[:], offsets).then_inc(ids_loaded, 16)
            for g in range(GROUPS):
                rows, j, end = group(g)
                sp.dma_start(w0_sb[rows, 0:end - j, :], w0a[j:end].rearrange("c i s -> i c s")).then_inc(w0_loaded, 16)
            sp.wait_ge(w0b_zeroed, 1)
            for g in range(GROUPS):
                rows, j, end = group(g)
                first = 1 if g == 0 else 0
                sp.dma_start(w0b_staged[rows, first:end - j, :],
                             w0b[j + first:end].rearrange("c i s -> i c s")).then_inc(w0b_loaded, 16)
            for i, w, w_staged, w_sb, loaded in ((1, w1, w1_staged, w1_sb, w1_loaded),
                                                 (2, w2, w2_staged, w2_sb, w2_loaded)):
                whole = w[0:(C1 - 1) * P, :].rearrange("(c p) s -> p c s", p=P)
                sp.dma_start(w_staged, whole[:, 0:SPLIT[i], :]).then_inc(loaded, 16)
                sp.dma_start(w_sb[:, :, :], whole[:, SPLIT[i]:, :]).then_inc(loaded, 16)
                for g in range(2):
                    sp.dma_start(ws_staged[HALF * g:HALF * (g + 1), i - 1, :], w[(C1 - 1) * P:, :]
                                 ).then_inc(ws_loaded, 16)
            for b, b_sb in ((b0, b0_sb), (b1, b1_sb), (b2, b2_sb)):
                sp.dma_start(b_sb[:], b.rearrange("(s a) -> s a", a=1)).then_inc(biases_loaded, 16)

            def write_x0(tile):
                sp.wait_ge(leaving_ready, tile + 1)
                for r in reversed(range(GROUPS)):
                    n = DIM * (SLOTS if r < GROUPS - 1 else LAST_SLOTS)
                    sp.dma_start(x0_rows(tile, r * SLOTS * DIM, [[TILE, FIELDS], [FIELDS * TILE, 2], [1, n]]),
                                 leaving[FIELDS * r:FIELDS * (r + 1), 0:n].unsqueeze(1).to_broadcast([FIELDS, 2, n])
                                 ).then_inc(x0_written, 16)

            def load_rotations(t):
                sp.dma_start(x0_rep[:, :], x0_rows(t, 0, [[0, GROUPS], [TILE, FIELDS], [1, TILE]])
                             ).then_inc(rep_loaded, 16)
                for unit, c, end in (("0a", 0, SPLIT[0]), ("0b", SPLIT[0], C0 - 1), ("0b", C0 - 1, C0)):
                    rows = C0_ROWS[c]
                    sp.dma_start(x0_rot[0:rows, c:end, :],
                                 x0_rows(t, c * TILE, [[C0 * TILE, rows // FIELDS], [TILE, FIELDS],
                                                       [1, (end - c) * TILE]])
                                 ).then_inc(rot_loaded[unit], 16)

            def load_spread(t, letter):
                c, end = SPREAD[letter]
                if end == C1:
                    end -= 1
                    sp.dma_start(x0_spread[:, end, :], x0_rows(t, end * TILE, [[0, P], [1, TILE]])
                                 ).then_inc(spread_loaded[letter], 16)
                sp.dma_start(x0_spread[:, c:end, :],
                             x0_rows(t, c * TILE, [[C1 * TILE, 2], [0, HALF], [1, (end - c) * TILE]])
                             ).then_inc(spread_loaded[letter], 16)

            def reload_spread(t, letter):
                sp.wait_ge(prod_ready, count(FORMED, t, "2" + letter))
                load_spread(t + 1, letter)

            def reload_rotations(t, turn, ahead):
                sp.wait_ge(prod_ready, count(FORMED, turn, "0b"))
                sp.wait_ge(x0_written, 16 * GROUPS * t + 16 * GROUPS * (ahead + 1))
                load_rotations(t + ahead)

            write_x0(0)
            sp.wait_ge(x0_written, 16 * GROUPS)
            load_rotations(0)
            for letter in SPREAD:
                load_spread(0, letter)
            write_x0(1)
            for i in range(3):
                sp.dma_start(ctx_sb[CTX * i:CTX * (i + 1)], ctx_t).then_inc(top_loaded, 16)
                sp.dma_start(wt1c_sb[CTX * i:CTX * (i + 1)], wt1[2 * P:, :]).then_inc(top_loaded, 16)
            for dst, src in ((wt1_sb[:], wt1[0:2 * P, :].rearrange("(c p) n -> p c n", p=P)),
                             (wt2_sb[:], wt2.rearrange("(c p) n -> p c n", p=P)),
                             (wt3_sb[:], wt3), (bt1_sb[:], bt1), (bt2_sb[:], bt2)):
                sp.dma_start(dst, src).then_inc(top_loaded, 16)
            reload_rotations(0, START, 1)

            def reload(t):
                for letter in "abcd":
                    reload_spread(t, letter)
                write_x0(t + 2)
                reload_spread(t, "e")
                reload_rotations(t, t, 2)

            with sp.Fori(0, TILES - 2) as t:
                reload(t)
            for letter in SPREAD:
                reload_spread(TILES - 2, letter)

            sp.wait_ge(y_ready, NH)
            sp.dma_start(out.rearrange("(h b) a -> a h b", h=NH), y).then_inc(out_written, 16)
            sp.wait_ge(out_written, 16)

        @block.vector
        def _(dve):
            dve.sem_inc(sum01_done, 1)
            dve.sem_inc(sum2_done, 1)
            nc.vector.memset(w0b_staged[:, 0, :], 0.0).then_inc(w0b_zeroed, 1)
            dve.wait_ge(w0_loaded, 16 * GROUPS)
            dve.wait_ge(w0b_loaded, 16 * GROUPS)
            nc.vector.tensor_tensor(w0_sb[:, 0:C0 - 1, :], w0_sb[:, 0:C0 - 1, :], w0b_staged[:, 0:C0 - 1, :],
                                    ALU.add).then_inc(w0_ready, 1)
            rows = C0_ROWS[C0 - 1]
            nc.vector.tensor_tensor(w0_sb[0:rows, C0 - 1, :], w0_sb[0:rows, C0 - 1, :], w0b_staged[0:rows, C0 - 1, :],
                                    ALU.add).then_inc(w0_ready, 1)
            for i, (w, w_hi, w_lo) in enumerate(((w0_sb[:, 0:SPLIT[0], :], w0_hi, w0_lo),
                                                 (w1_staged, w1_hi, w1_lo), (w2_staged, w2_hi, w2_lo),
                                                 (ws_staged[0:HALF], ws_hi[0:HALF], ws_lo))):
                dve.wait_ge(whi_ready, i + 1)
                nc.vector.tensor_tensor(w_lo[:], w, w_hi[:].bitcast(F32), ALU.subtract).then_inc(wlo_ready, 1)

            dve.wait_ge(wlo_ready, 4)

            def products(t, unit, chunk_rows, left, right, half=None):
                units = FORMED[0] if t is START else FORMED[1] + FORMED[2 if t is END else 1]
                place = len(units) - 1 - units[::-1].index(unit) - RING
                if place >= 0:
                    holder = units[place]
                    ago = int(t is not START and place < len(FORMED[1]))
                    if UNITS[holder][0] == NATIVE:
                        dve.wait_ge(used[NATIVE], count(TAKEN, t, holder, [NATIVE], ago))
                    elif UNITS[holder][0] == OWN:
                        dve.wait_ge(own_lo_ready, count(OWN_LOWS, t, holder, ago=ago))
                    else:
                        dve.wait_ge(pool_lo_ready, count(POOL_LOWS, t, holder, ago=ago))
                    if holder[1] == "e":
                        dve.wait_ge(own_lo_ready, count(OWN_LOWS, t, holder[0] + "s", ago=ago))
                _, first, end = UNITS[unit]
                end += unit[1] == "e"
                full = sum(chunk_rows[c] == chunk_rows[0] for c in range(first, end))
                parts = ((first, full), (first + full, end - first - full))
                if half is not None:
                    parts = ((first + half * UNIT // 2, UNIT // 2),)
                for c, m in parts:
                    if m:
                        rows = chunk_rows[c]
                        last = nc.vector.tensor_tensor(prod[0:rows, slot(t, unit), c - first:c - first + m, :],
                                                       left(rows, c, m), right(rows, c, m), ALU.mult)
                last.then_inc(half_ready if half == 0 else prod_ready, 1)

            def low_parts(t, unit, rows=P):
                _, first, end = UNITS[unit]
                dve.wait_ge(hi_ready, count(HIGHS, t, unit))
                nc.vector.tensor_tensor(own_lo[0:rows, 0:end - first, :], prod[0:rows, slot(t, unit), 0:end - first, :],
                                        own_hi[0:rows, 0:end - first, :].bitcast(F32), ALU.subtract
                                        ).then_inc(own_lo_ready, 1)

            def stacked_low_parts(t, unit):
                dve.wait_ge(hi_ready, count(HIGHS, t, unit))
                nc.vector.tensor_tensor(stacked[HALF:P, :], prod[HALF:P, slot(t, unit[0] + "e"), UNIT - 1, :],
                                        stacked[HALF:P, :].bitcast(F32), ALU.subtract).then_inc(own_lo_ready, 1)

            def same(x):
                return lambda rows, c, m: x[0:rows, :].unsqueeze(1).to_broadcast([rows, m, TILE])

            def chunks_of(x):
                return lambda rows, c, m: x[0:rows, c:c + m, :]

            def layer0(t, tile):
                dve.wait_ge(rep_ready, tile + 1)
                for unit in ("0a", "0b"):
                    dve.wait_ge(rot_loaded[unit], (16 if unit == "0a" else 32) * (tile + 1))
                    products(t, unit, C0_ROWS, chunks_of(x0_rot), same(rep_ps))
                low_parts(t, "0a", GP)

            def form(t, tile, unit, x, half=None):
                if x is x1:
                    letter = unit[1]
                    dve.wait_ge(spread_loaded[letter], (32 if letter == "e" else 16) * (tile + 1))
                products(t, unit, C1_ROWS, chunks_of(x0_spread), same(x), half)

            def form_first(t, tile):
                form(t, tile, "2a", x2, half=0)
                form(t, tile, "2b", x2)
                form(t, tile, "2a", x2, half=1)

            def sum_dims(z_out, src):
                return nc.vector.tensor_reduce(z_out, src.rearrange("p (b d) -> p b d", d=DIM), AX_X, ALU.add)

            def sum01(t):
                dve.wait_ge(direct0_ready, t + 1)
                dve.wait_ge(direct1_ready, t + 1)
                sum_dims(z[:, 0, bass.ds(t * SAMPLES, SAMPLES)], direct01[:, :]).then_inc(sum01_done, 1)

            def sum2(t):
                dve.wait_ge(direct2_ready, t + 2)
                sum_dims(z[:, 1, bass.ds(t * SAMPLES, SAMPLES)], direct2[:, :]).then_inc(sum2_done, 1)

            layer0(START, 0)
            dve.wait_ge(x1_ready, 2)
            for unit in ("1a", "1b", "1c", "1d"):
                form(START, 0, unit, x1)
            low_parts(START, "1c")
            form(START, 0, "1e", x1)
            stacked_low_parts(START, "1s")
            dve.wait_ge(pool_lo_ready, 1)
            with dve.Fori(0, TILES - 1) as t:
                layer0(t, t + 1)
                dve.wait_ge(x2_ready, 2 * (t + 1))
                form_first(t, t)
                form(t, t, "2c", x2)
                form(t, t, "2d", x2)
                sum01(t)
                dve.wait_ge(x1_ready, 2 * (t + 2))
                form(t, t + 1, "1a", x1)
                form(t, t + 1, "1b", x1)
                form(t, t, "2e", x2)
                form(t, t + 1, "1c", x1)
                stacked_low_parts(t, "2s")
                form(t, t + 1, "1d", x1)
                low_parts(t, "1c")
                form(t, t + 1, "1e", x1)
                sum2(t)
                stacked_low_parts(t, "1s")
            last = TILES - 1

            def low(dst, src, hi):
                return nc.vector.tensor_tensor(dst, src, hi.bitcast(F32), ALU.subtract)

            def z_low_parts(i):
                cols = Z_COLS[i]
                dve.wait_ge(z_hi_ready, i + 1)
                low(z_lo[:, :, cols], z[:, :, cols], z_hi[:, :, cols]).then_inc(z_lo_ready, 1)

            dve.wait_ge(top_hi_ready, 1)
            low(wt1c_parts[0:2 * CTX, :], wt1c_sb[0:2 * CTX, :], wt1c_hi[0:2 * CTX, :]).then_inc(top_lo_ready, 1)
            dve.wait_ge(top_hi_ready, 2)
            rows = slice(2 * CTX, 3 * CTX)
            low(ctx_parts[rows, :], ctx_sb[rows, :], ctx_parts[rows, :]).then_inc(top_lo_ready, 1)
            dve.wait_ge(top_hi_ready, 5)
            low(wt1_lo, wt1_sb[:], wt1_hi).then_inc(top_lo_ready, 1)
            z_low_parts(0)

            dve.wait_ge(x2_ready, 2 * TILES)
            form_first(END, last)
            for unit in ("2d", "2c", "2e"):
                form(END, last, unit, x2)
            stacked_low_parts(END, "2s")
            sum01(last)

            def h1_low_parts(n):
                for m in range(M1):
                    dve.wait_ge(h1_hi_ready, 2 * (M1 * n + m + 1))
                    low(h1_lo[n][:, m, :], h1[:, m, :], h1_hi[n][:, m, :]).then_inc(h1_lo_ready, 1)

            h1_low_parts(0)
            dve.wait_ge(top_hi_ready, 6)
            low(wt2_lo, wt2_sb[:], wt2_hi).then_inc(top_lo_ready, 1)
            z_low_parts(1)
            sum2(last)
            z_low_parts(2)
            h1_low_parts(1)
            for n in range(NH):
                dve.wait_ge(y_done, n + 1)
                nc.vector.tensor_copy(y[:, n, :], ps[0:1, BANKS3[n], :]).then_inc(y_ready, 1)

        @block.tensor
        def _(pe):
            LAYERS = ((C0_ROWS, w0_sb, 0, w0_hi, w0_lo, ps0),
                      (C1_ROWS, w1_sb, SPLIT[1], w1_hi, w1_lo, ps1),
                      (C1_ROWS, w2_sb, SPLIT[2], w2_hi, w2_lo, ps2))

            def contract(t, unit):
                layer = int(unit[0])
                chunk_rows, w_native, native_first, w_hi, w_lo, out_ps = LAYERS[layer]
                of_layer = [u for u in TAKEN[0 if t is START else 2 if t is END else 1] if u[0] == unit[0]]
                start, stop = unit == of_layer[0], unit == of_layer[-1]
                kind, first, end = UNITS[unit]
                if unit == "2a":
                    pe.wait_ge(half_ready, TILES if t is END else t + 1)
                elif kind == NATIVE:
                    pe.wait_ge(prod_ready, count(FORMED, t, unit))
                elif kind == POOL:
                    pe.wait_ge(pool_lo_ready, count(POOL_LOWS, t, unit))
                else:
                    pe.wait_ge(own_lo_ready, count(OWN_LOWS, t, unit))
                if kind == STACKED:
                    nc.tensor.matmul(out_ps, ws_hi[:, layer - 1, :], stacked[:, :], start=start, stop=False)
                    mm = nc.tensor.matmul(out_ps, ws_lo[:, layer - 1, :], stacked[0:HALF, :], start=False, stop=stop)
                    mm.then_inc(used[STACKED], 1)
                    return
                i = (count(POOL_LOWS, t if t is START or t is END else 0, unit) - 1) % POOL_RING if kind == POOL else 0
                for c in range(first, end):
                    rows = slice(0, chunk_rows[c])
                    begin, finish = start and c == first, stop and c == end - 1
                    if unit == "2a" and c == first + UNIT // 2:
                        pe.wait_ge(prod_ready, count(FORMED, t, unit))
                    if kind == NATIVE:
                        mm = nc.tensor.matmul(out_ps, w_native[rows, c - native_first, :],
                                              prod[rows, slot(t, unit), c - first, :], start=begin, stop=finish)
                    else:
                        hi, lo = ((own_hi[rows, c - first, :], own_lo[rows, c - first, :]) if kind == OWN else
                                  (pool_hi[rows, i, c - first, :], pool_lo[rows, i, c - first, :]))
                        nc.tensor.matmul(out_ps, w_hi[rows, c, :], lo, start=begin, stop=False)
                        nc.tensor.matmul(out_ps, w_lo[rows, c, :], hi, start=False, stop=False)
                        mm = nc.tensor.matmul(out_ps, w_hi[rows, c, :], hi, start=False, stop=finish)
                mm.then_inc(used[kind], 1)

            pe.wait_ge(w0_ready, 2)
            pe.wait_ge(wlo_ready, 4)
            pe.wait_ge(w1_loaded, 32)
            pe.wait_ge(w2_loaded, 32)

            def keep_busy(n):
                for _ in range(n):
                    nc.tensor.matmul(ps[:, 6, :], w0_sb[:, 0, :], w0_sb[:, 0:TILE // SIZE, :].rearrange(
                        "p c s -> p (c s)"), start=True, stop=True)

            pe.wait_ge(x0_written, 16 * GROUPS)
            keep_busy(9)
            for unit in TAKEN[0]:
                if unit == "1a":
                    keep_busy(4)
                elif unit == "1b":
                    keep_busy(5)
                contract(START, unit)
            with pe.Fori(0, TILES - 1) as t:
                for unit in TAKEN[1]:
                    if unit == "0b":
                        pe.wait_ge(direct0_ready, t + 1)
                    elif unit == "2a":
                        pe.wait_ge(direct2_ready, t + 1)
                    elif unit == "1a":
                        pe.wait_ge(direct1_ready, t + 1)
                    contract(t, unit)

            def mlp1(n):
                cols = slice(BANK * n, BANK * (n + 1))
                for m in range(M1):
                    outs = slice(P * m, P * (m + 1))
                    bank = ps[:, BANKS1[n][m], :]
                    for c in range(2):
                        nc.tensor.matmul(bank, wt1_hi[:, c, outs], z_lo[:, c, cols], start=(c == 0), stop=False)
                        nc.tensor.matmul(bank, wt1_lo[:, c, outs], z_hi[:, c, cols], start=False, stop=False)
                        nc.tensor.matmul(bank, wt1_hi[:, c, outs], z_hi[:, c, cols], start=False, stop=False)
                    nc.tensor.matmul(bank, wt1c_parts[:, outs], ctx_parts[:, cols],
                                     start=False, stop=True).then_inc(h1_done, 1)

            def mlp2(n):
                for m in range(M2):
                    outs = slice(P * m, P * (m + 1))
                    bank = ps[:, BANKS2[n][m], :]
                    for c in range(M1):
                        pe.wait_ge(h1_lo_ready, M1 * n + (M1 if n == 0 else c + 1))
                        nc.tensor.matmul(bank, wt2_hi[:, c, outs], h1_lo[n][:, c, :], start=(c == 0), stop=False)
                        nc.tensor.matmul(bank, wt2_lo[:, c, outs], h1_hi[n][:, c, :], start=False, stop=False)
                        mm = nc.tensor.matmul(bank, wt2_hi[:, c, outs], h1_hi[n][:, c, :],
                                              start=False, stop=(c == M1 - 1))
                    mm.then_inc(h2_done, 1)

            def mlp3(n):
                for c in range(M2):
                    pe.wait_ge(h2_ready, M2 * n + c + 1)
                    mm = nc.tensor.matmul(ps[0:1, BANKS3[n], :], wt3_sb[:, c:c + 1], h2[:, c, n, :],
                                          start=(c == 0), stop=(c == M2 - 1))
                mm.then_inc(y_done, 1)

            pe.wait_ge(z_lo_ready, 1)
            pe.wait_ge(top_lo_ready, 3)
            pe.wait_ge(top_hi_ready, 5)
            mlp1(0)
            pe.wait_ge(direct2_ready, TILES)
            for unit in TAKEN[2]:
                contract(END, unit)

            pe.wait_ge(top_lo_ready, 4)
            mlp2(0)
            pe.wait_ge(z_lo_ready, 3)
            mlp1(1)
            mlp3(0)
            mlp2(1)
            mlp3(1)

        @block.scalar
        def _(act):
            def relu(dst, src, bias):
                return nc.scalar.activation(dst, src, ACT.Relu, bias=bias)

            def copy(dst, src):
                return nc.scalar.activation(dst, src, ACT.Copy)

            LOW, HIGH = slice(0, HALF), slice(HALF, SIZE)

            def high_parts(t, unit, rows=P):
                kind, first, end = UNITS[unit]
                formed = unit[0] + "e" if kind == STACKED else unit
                act.wait_ge(prod_ready, count(FORMED, t, formed))
                ring = POOL_RING if kind == POOL else 1
                n = count(TAKEN, t if t is START or t is END else 0, unit, [kind])
                if n > ring:
                    act.wait_ge(used[kind], count(TAKEN, t, unit, [kind]) - ring)
                if kind == STACKED:
                    dst, src = stacked[:, :], prod[:, slot(t, formed), UNIT - 1, :]
                else:
                    hi = own_hi if kind == OWN else pool_hi[:, (n - 1) % POOL_RING, :, :]
                    dst, src = hi[0:rows, 0:end - first, :], prod[0:rows, slot(t, unit), 0:end - first, :]
                copy(dst, src).then_inc(hi_ready, 1)

            def take_x0(tile, first=False):
                act.wait_ge(tile_gathered, 16 * SLOTS * (tile + 1))
                if not first:
                    act.wait_ge(x0_written, 16 * GROUPS * tile)
                copy(leaving[:], gathered[:]).then_inc(leaving_ready, 1)

            def copy_rep(tile):
                act.wait_ge(rep_loaded, 16 * (tile + 1))
                copy(rep_ps, x0_rep[:, :]).then_inc(rep_ready, 1)

            def next_factor(out_ps, bias, x, x_ready):
                for half in (LOW, HIGH):
                    relu(x[half, :], out_ps[LOW, :], bias[LOW, :]).then_inc(x_ready, 1)

            def direct_outputs(tile, out_ps, bias, direct, direct_ready):
                act.wait_ge(sum01_done, tile + 1)
                relu(direct, out_ps[HIGH, :], bias[HIGH, :]).then_inc(direct_ready, 1)

            def factor1(t):
                act.wait_ge(used[OWN], count(TAKEN, t, "0a", [OWN]))
                next_factor(ps0, b0_sb, x1, x1_ready)

            def direct0(tile):
                direct_outputs(tile, ps0, b0_sb, direct01[LOW, :], direct0_ready)

            def outputs1(t, tile):
                act.wait_ge(used[STACKED], count(TAKEN, t, None, [STACKED]))
                next_factor(ps1, b1_sb, x2, x2_ready)
                direct_outputs(tile, ps1, b1_sb, direct01[HIGH, :], direct1_ready)

            def outputs2(t, tile):
                act.wait_ge(used[STACKED], count(TAKEN, t, "2s", [STACKED]))
                act.wait_ge(sum2_done, tile + 1)
                relu(direct2[:, :], ps2, b2_sb[:, :]).then_inc(direct2_ready, 1)

            act.sem_inc(direct2_ready, 1)
            act.wait_ge(w0_ready, 1)
            copy(w0_hi[:], w0_sb[:, 0:SPLIT[0], :]).then_inc(whi_ready, 1)
            act.wait_ge(w1_loaded, 32)
            copy(w1_hi[:], w1_staged).then_inc(whi_ready, 1)
            act.wait_ge(w2_loaded, 32)
            copy(w2_hi[:], w2_staged).then_inc(whi_ready, 1)
            act.wait_ge(ws_loaded, 64)
            copy(ws_hi[:], ws_staged).then_inc(whi_ready, 1)
            act.wait_ge(biases_loaded, 16 * 3)

            take_x0(0, first=True)
            copy_rep(0)
            high_parts(START, "0a", GP)
            factor1(START)
            direct0(0)
            high_parts(START, "1b")
            take_x0(1)
            for unit in ("1c", "1d", "1s"):
                high_parts(START, unit)

            def turn(t, writes):
                copy_rep(t + 1)
                high_parts(t, "0a", GP)
                outputs1(t, t)
                high_parts(t, "2b")
                if writes:
                    take_x0(t + 2)
                factor1(t)
                high_parts(t, "2d")
                direct0(t + 1)
                high_parts(t, "1b")
                high_parts(t, "2s")
                high_parts(t, "1c")
                high_parts(t, "1d")
                outputs2(t, t)
                high_parts(t, "1s")

            with act.Fori(0, TILES - 2) as t:
                turn(t, True)
            turn(TILES - 2, False)

            act.wait_ge(top_loaded, 16 * TOP_LOADS)
            copy(wt1c_hi, wt1c_sb[:]).then_inc(top_hi_ready, 1)
            copy(ctx_parts[:, :], ctx_sb[:]).then_inc(top_hi_ready, 1)
            act.wait_ge(top_lo_ready, 1)
            for rows in (slice(0, CTX), slice(2 * CTX, 3 * CTX)):
                copy(wt1c_parts[rows, :], wt1c_hi[rows, :].bitcast(F32)).then_inc(top_hi_ready, 1)
            act.wait_ge(used[OWN], count(TAKEN, END, None, [OWN]))
            copy(wt1_hi, wt1_sb[:]).then_inc(top_hi_ready, 1)

            def z_high_parts(cols):
                copy(z_hi[:, :, cols], z[:, :, cols]).then_inc(z_hi_ready, 1)

            act.wait_ge(sum01_done, TILES)
            act.wait_ge(sum2_done, TILES)
            z_high_parts(Z_COLS[0])

            def h1_outputs(n, m):
                act.wait_ge(h1_done, M1 * n + m + 1)
                if n:
                    act.wait_ge(h1_lo_ready, M1)
                for dst in (h1, h1_hi[n]):
                    relu(dst[:, m, :], ps[:, BANKS1[n][m], :], bt1_sb[:, m:m + 1]).then_inc(h1_hi_ready, 1)

            def h2_outputs(n):
                for m in range(M2):
                    act.wait_ge(h2_done, M2 * n + m + 1)
                    relu(h2[:, m, n, :], ps[:, BANKS2[n][m], :], bt2_sb[:, m:m + 1]).then_inc(h2_ready, 1)

            outputs1(END, TILES - 1)
            z_high_parts(Z_COLS[1])
            high_parts(END, "2b")
            h1_outputs(0, 0)
            high_parts(END, "2d")
            h1_outputs(0, 1)
            h1_outputs(0, 2)
            high_parts(END, "2s")
            h1_outputs(0, 3)
            act.wait_ge(used[POOL], count(TAKEN, END, "2b", [POOL]))
            copy(wt2_hi, wt2_sb[:]).then_inc(top_hi_ready, 1)
            outputs2(END, TILES - 1)
            act.wait_ge(sum01_done, TILES + 1)
            act.wait_ge(sum2_done, TILES + 1)
            z_high_parts(Z_COLS[2])
            h2_outputs(0)
            for m in range(M1):
                h1_outputs(1, m)
            h2_outputs(1)


def kernel(**inputs):
    import numpy as np
    import concourse.bacc as bacc
    from concourse.bass_utils import run_bass_kernel_spmd

    a = {k: np.asarray(v) for k, v in inputs.items()}
    tables = [a[f"tbl_{f}"] for f in range(FIELDS)]
    starts = np.cumsum([0] + [t.shape[0] for t in tables[:-1]]).astype(np.int32)

    sample = np.minimum(np.arange(GROUPS)[:, None] * SLOTS + np.arange(SLOTS)[None, :], SAMPLES - 1)
    ids = a["ids"].reshape(TILES, SAMPLES, FIELDS)[:, sample, :]
    ids = ids.transpose(1, 3, 0, 2).reshape(GP, TILES * SLOTS)
    offsets = np.broadcast_to(np.tile(starts, GROUPS)[:, None], (GP, SLOTS))

    i = np.arange(FIELDS)[None, :]
    k = (i + np.arange(ROTATIONS)[:, None]) % FIELDS
    w0 = a["L0_rec_w0"]
    pairs = [f for c in range(C1) for f in range(c, FIELDS, C1)]
    host = {
        "table": np.concatenate(tables, axis=0),
        "ids": ids, "offsets": offsets,
        "ctx_t": a["dense_ctx"].T,
        "w0a": w0[i, k], "w0b": w0[k, i],
        "w1": a["L0_rec_w1"].reshape(FIELDS, HALF, SIZE)[pairs].reshape(FIELDS * HALF, SIZE),
        "w2": a["L0_rec_w2"].reshape(FIELDS, HALF, SIZE)[pairs].reshape(FIELDS * HALF, SIZE),
        "b0": a["L0_rec_b0"], "b1": a["L0_rec_b1"], "b2": a["L0_rec_b2"],
        "wt1": a["W_top1"], "bt1": a["b_top1"].reshape(M1, P).T,
        "wt2": a["W_top2"], "bt2": a["b_top2"].reshape(M2, P).T,
        "wt3": a["W_top3"].reshape(M2, P).T,
    }
    host = {k_: np.ascontiguousarray(v) for k_, v in host.items()}
    nc = bacc.Bacc("TRN2", target_bir_lowering=False, num_devices=1)
    args = [nc.dram_tensor(k_, v.shape, mybir.dt.from_np(v.dtype), kind="ExternalInput").ap() for k_, v in host.items()]
    args.append(nc.dram_tensor("out", (BATCH, 1), F32, kind="ExternalOutput").ap())
    tower(nc, *args)
    result = run_bass_kernel_spmd(nc, [host], core_ids=[0])
    return result.results[0]["out"]
```
